# Optimizing a Trainium2 kernel written in Bass

```python
import numpy as np
import jax
import jax.numpy as jnp

def _softmax(x, axis=-1):
    return jax.nn.softmax(x, axis=axis)

def _gelu(x):
    return jax.nn.gelu(x, approximate=True)

def _silu(x):
    return jax.nn.silu(x)

def _sigmoid(x):
    return jax.nn.sigmoid(x)

def _layernorm(x, axis=-1, eps=1e-05):
    m = jnp.mean(x, axis=axis, keepdims=True)
    v = jnp.var(x, axis=axis, keepdims=True)
    return (x - m) / jnp.sqrt(v + eps)

def _scatter_add(tgt, idx, src, axis=0):
    return tgt.at[idx].add(src)

def _segment_sum(src, seg, n):
    return jax.ops.segment_sum(src, seg, n)
kernel_name = 'mk_gnn_preln_d2_gnn_r64_fec763'

def setup_inputs(seed: int=0):
    np.random.seed(seed)
    _w = jnp.asarray

    def _rec_inputs():
        import jax
        import jax.numpy as jnp
        _gk = jax.random.key(seed)
        x = -0.000202 + 1 * jax.random.normal(jax.random.fold_in(_gk, 1), (100000, 128), jnp.float32)
        src = jax.random.randint(jax.random.fold_in(_gk, 2), (50000,), 0, 100000, jnp.int32)
        dst = jax.random.randint(jax.random.fold_in(_gk, 3), (50000,), 0, 100000, jnp.int32)
        _o = jnp.argsort(dst, stable=True)
        src = src[_o]
        dst = dst[_o]
        edge_attr_16 = 0.000254156 + 0.999948 * jax.random.normal(jax.random.fold_in(_gk, 12), (50000, 16), jnp.float32)
        edge_weight = 0.00176116 + 0.999358 * jax.random.normal(jax.random.fold_in(_gk, 14), (50000,), jnp.float32)
        return (x, src, dst, edge_attr_16, edge_weight)
    x, src, dst, edge_attr_16, edge_weight = _rec_inputs()

    def _L0_gnn_setup():
        import jax, jax.numpy as jnp
        import numpy as np
        N, E, D_IN, D_H, D_E, L = (50000, 12500, 128, 128, 16, 3)
        LN_EPS = 1e-05
        key = jax.random.key(seed)
        ks = jax.random.split(key, 8)
        x = jax.random.normal(ks[0], (N, D_IN), jnp.float32)
        edge_index = jax.random.randint(ks[1], (2, E), 0, N, jnp.int32)
        edge_attr = jax.random.normal(ks[2], (E, D_E), jnp.float32)
        s = lambda d: 1.0 / np.sqrt(d)
        lin_w = jax.random.normal(ks[3], (L, D_IN, D_H), jnp.float32) * s(D_IN)
        edge_w1 = jax.random.normal(ks[4], (L, D_E, D_H), jnp.float32) * s(D_E)
        edge_b1 = jnp.zeros((L, D_H), jnp.float32)
        edge_w2 = jax.random.normal(ks[5], (L, D_H, D_H), jnp.float32) * s(D_H)
        edge_b2 = jnp.zeros((L, D_H), jnp.float32)
        bias = jnp.zeros((L, D_H), jnp.float32)
        ln_w = jnp.ones((L, D_H), jnp.float32)
        ln_b = jnp.zeros((L, D_H), jnp.float32)
        return dict(x=x, edge_attr=edge_attr, lin_w=lin_w, edge_w1=edge_w1, edge_b1=edge_b1, edge_w2=edge_w2, edge_b2=edge_b2, bias=bias, ln_w=ln_w, ln_b=ln_b, edge_index=edge_index)
    _L0_gnn_all = _L0_gnn_setup()
    _L0_gnn_in = {k: v for k, v in _L0_gnn_all.items() if k in ('lin_w', 'edge_w1', 'edge_b1', 'edge_w2', 'edge_b2', 'bias', 'ln_w', 'ln_b')}
    del _L0_gnn_all

    def _L1_gnn_setup():
        import jax, jax.numpy as jnp
        import numpy as np
        N_NODES = 50000
        N_PAIRS = 625000
        F = 128
        key = jax.random.key(seed)
        k1, k2, k3, k4, k5 = jax.random.split(key, 5)
        x = jax.random.normal(k1, (N_NODES, F), dtype=jnp.float32)
        alpha_ij = jax.random.normal(k2, (N_PAIRS,), dtype=jnp.float32)
        idx_i = jax.random.randint(k3, (N_PAIRS,), 0, N_NODES, dtype=jnp.int32)
        idx_j = jax.random.randint(k4, (N_PAIRS,), 0, N_NODES, dtype=jnp.int32)
        W = jax.random.normal(k5, (F, F), dtype=jnp.float32) / np.sqrt(F)
        return {'x': x, 'alpha_ij': alpha_ij, 'idx_i': idx_i, 'idx_j': idx_j, 'W': W}
    _L1_gnn_all = _L1_gnn_setup()
    _L1_gnn_in = {k: v for k, v in _L1_gnn_all.items() if k in ('W',)}
    del _L1_gnn_all
    return {'x': x, 'src': src, 'dst': dst, 'edge_attr_16': edge_attr_16, 'edge_weight': edge_weight, 'L0_gnn_lin_w': _L0_gnn_in['lin_w'], 'L0_gnn_edge_w1': _L0_gnn_in['edge_w1'], 'L0_gnn_edge_b1': _L0_gnn_in['edge_b1'], 'L0_gnn_edge_w2': _L0_gnn_in['edge_w2'], 'L0_gnn_edge_b2': _L0_gnn_in['edge_b2'], 'L0_gnn_bias': _L0_gnn_in['bias'], 'L0_gnn_ln_w': _L0_gnn_in['ln_w'], 'L0_gnn_ln_b': _L0_gnn_in['ln_b'], 'L1_gnn_W': _L1_gnn_in['W']}

def reference(x, src, dst, edge_attr_16, edge_weight, L0_gnn_lin_w, L0_gnn_edge_w1, L0_gnn_edge_b1, L0_gnn_edge_w2, L0_gnn_edge_b2, L0_gnn_bias, L0_gnn_ln_w, L0_gnn_ln_b, L1_gnn_W):
    import jax
    import jax.numpy as jnp

    def _L0_gnn_ref(x, edge_attr, lin_w, edge_w1, edge_b1, edge_w2, edge_b2, bias, ln_w, ln_b, edge_index):
        import jax, jax.numpy as jnp
        import numpy as np
        N, E, D_IN, D_H, D_E, L = (50000, 12500, 128, 128, 16, 3)
        LN_EPS = 1e-05
        row, col = (edge_index[0], edge_index[1])
        n = x.shape[0]
        deg = jax.ops.segment_sum(jnp.ones(row.shape, x.dtype), col, num_segments=n)
        dis = jnp.where(deg > 0, jax.lax.rsqrt(jnp.maximum(deg, 1e-30)), 0.0)
        w = dis[row] * dis[col]
        h = x
        for l in range(L):
            hx = h @ lin_w[l]
            ea = jax.nn.relu(edge_attr @ edge_w1[l] + edge_b1[l]) @ edge_w2[l] + edge_b2[l]
            msg = hx[row] * w[:, None] + ea
            out = jax.ops.segment_sum(msg, col, num_segments=n) + bias[l]
            mu = out.mean(-1, keepdims=True)
            var = ((out - mu) ** 2).mean(-1, keepdims=True)
            h = jax.nn.relu((out - mu) * jax.lax.rsqrt(var + LN_EPS) * ln_w[l] + ln_b[l])
        return h

    def _L1_gnn_ref(x, alpha_ij, idx_i, idx_j, W):
        import jax, jax.numpy as jnp
        import numpy as np
        N_NODES = 50000
        N_PAIRS = 625000
        F = 128
        v = jnp.matmul(x, W)
        msg = alpha_ij[:, None] * v[idx_j]
        return jax.ops.segment_sum(msg, segment_ids=idx_i, num_segments=x.shape[0])
    edge_index = jnp.stack([src, dst])
    h = jnp.maximum(_layernorm(x, axis=-1), 0.0)
    x = x + _L0_gnn_ref(h, edge_attr_16, L0_gnn_lin_w, L0_gnn_edge_w1, L0_gnn_edge_b1, L0_gnn_edge_w2, L0_gnn_edge_b2, L0_gnn_bias, L0_gnn_ln_w, L0_gnn_ln_b, edge_index)
    h = jnp.maximum(_layernorm(x, axis=-1), 0.0)
    x = x + _L1_gnn_ref(h, edge_weight, src, dst, L1_gnn_W)
    return x

_drawn_inputs = setup_inputs


def setup_inputs(seed=0):
    import zlib

    import numpy as np

    out = dict(_drawn_inputs(seed))
    spreads = {'L0_gnn_edge_b1': (0.0, 0.1),
     'L0_gnn_edge_b2': (0.0, 0.1),
     'L0_gnn_bias': (0.0, 0.1),
     'L0_gnn_ln_w': (1.0, 0.2),
     'L0_gnn_ln_b': (0.0, 0.1)}
    factors = {}
    for name, (base, spread) in spreads.items():
        noise = np.random.default_rng([zlib.crc32(name.encode()), seed]).standard_normal(out[name].shape)
        drawn = base * np.exp(spread * noise) if base else spread * noise
        out[name] = jnp.asarray(drawn.astype(out[name].dtype))
    for name, factor in factors.items():
        out[name] = (out[name] * factor).astype(out[name].dtype)
    return out
```

```python
import concourse.bass as bass
from concourse import mybir
from contextlib import ExitStack

N = 100000
E = 50000
D = 128
DE = 16
LAYERS = 3
P = 128
GT = 4
GROUPS = -(-E // (P * GT))
ITERS = GROUPS // 2
TILES = GROUPS * GT
EP = TILES * P
GE = GT * P
DUMP = N + 1
ROWS_OUT = DUMP + GE
SKIP = 2 * N
LN_EPS = 1e-5
FAR = 2.0 * EP
RP, CR = 780, 13
CHUNKS = RP // CR
REST = N - P * RP
CW = CR * D
TQ = TILES // GT


class Count:

    def __init__(self, sem, per=1, credit=None):
        self.sem, self.per = sem, per
        self.credit = 2 * per if credit is None else credit

    def done(self, n, k=None):
        return n * self.per + (self.credit + (self.per if k is None else k))

    def free(self, n):
        return n * self.per + (self.credit - self.per)


def gnn(nc, t):
    f32, i32 = mybir.dt.float32, mybir.dt.int32
    ALU, ACT = mybir.AluOpType, mybir.ActivationFunctionType
    ctx = ExitStack()
    with ctx:
        def sb(name, shape, dt=f32):
            return ctx.enter_context(nc.sbuf_tensor(name, shape, dt))

        def ps(name):
            return ctx.enter_context(nc.psum_tensor(name, [P, GE], f32))

        def sem(name):
            return ctx.enter_context(nc.semaphore(name))

        ident = sb("ident", [P, P])
        lin_w = sb("lin_w", [P, LAYERS * D])
        edge_w2 = sb("edge_w2", [P, LAYERS * D])
        edge_w1 = sb("edge_w1", [DE + 1, LAYERS * D])
        out_w = sb("out_w", [P, D])
        ln_w = sb("ln_w", [P, LAYERS * D])
        ln_b = sb("ln_b", [P, LAYERS * D])
        last_bias = sb("last_bias", [P, D])
        carry = sb("carry", [3, LAYERS * D])
        zeros = sb("zeros", [P, 2000])
        dst_b = sb("dst_b", [P, TILES], i32)
        dst_b_prev = sb("dst_b_prev", [P, TILES], i32)
        dst_b_next = sb("dst_b_next", [P, TILES], i32)
        pos_b = sb("pos_b", [P, 3 * TILES])
        is_head_b = sb("is_head_b", [P, TILES])
        is_tail_b = sb("is_tail_b", [P, TILES])
        head_b = sb("head_b", [P, TILES])
        tail_b = sb("tail_b", [P, TILES])
        deg_b = sb("deg_b", [P, TILES])
        dis_b = sb("dis_b", [P, TILES])
        root_b = sb("root_b", [P, TILES])
        goes_on_b = sb("goes_on_b", [P, TILES])
        bias_row_b = sb("bias_row_b", [P, TILES])
        b2_row_b = sb("b2_row_b", [P, TILES])
        tmp_b = sb("tmp_b", [P, TILES])
        node_idx_b = sb("node_idx_b", [P, TILES], i32)
        node_row_b = sb("node_row_b", [P, 2 * TILES])
        seam = sb("seam", [P, 4])
        seam_row = sb("seam_row", [1, 4 * P])
        src_a = sb("src_a", [P, TILES], i32)
        dst_a = sb("dst_a", [P, TILES], i32)
        dst_a_prev = sb("dst_a_prev", [P, TILES], i32)
        dump_a = sb("dump_a", [P, TILES])
        ew_a = sb("ew_a", [P, TILES])
        is_head_a = sb("is_head_a", [P, TILES])
        tmp_a = sb("tmp_a", [P, TILES])
        src_f = sb("src_f", [P, TILES])
        cols = sb("cols", [P, TILES * 4])
        cols_out = sb("cols_out", [P, TILES * 4])
        own = sb("own", [P, 2 * TILES])
        src_row_idx = sb("src_row_idx", [P, TILES], i32)
        x1_idx = sb("x1_idx", [P, TILES], i32)
        add_idx = sb("add_idx", [P, TILES], i32)
        earlier = sb("earlier", [P, TILES])
        before = sb("before", [P, GT * GE])
        dis_t = sb("dis_t", [TQ, GT * P])
        first_head = sb("first_head", [TQ, GT])
        first_idx = sb("first_idx", [TQ, GT], i32)
        first_v = sb("first_v", [TQ, GT * D])
        attr_s = sb("attr_s", [P, EP // 8])
        root_s = sb("root_s", [P, EP // 8])
        y, ho, x1, v_in, zz = (root_s[:, k * 2 * GE:(k + 1) * 2 * GE] for k in range(5))
        xin = sb("xin", [P, 2 * CW])
        xout = sb("xout", [P, 2 * CW])
        base = sb("base", [P, D])
        stage_idx = sb("stage_idx", [P, 2 * GT], i32)
        stage_idx2 = sb("stage_idx2", [P, 2 * GT], i32)
        stage_idx3 = sb("stage_idx3", [P, 2 * GT], i32)
        stage_row = sb("stage_row", [P, 2 * 2 * GT])
        stage_cols = sb("stage_cols", [P, 2 * 4 * GT])
        gat = sb("gat", [P, 2 * GE])
        rows = sb("rows", [P, 2 * GE], i32)
        rows_src = sb("rows_src", [P, 2 * GE], i32)
        attr = sb("attr", [DE + 1, 2 * GE])
        rank3 = sb("rank3", [3, 2 * GE])
        eq = sb("eq", [P, 2 * GE])
        same_src = attr_s
        rT = sb("rT", [P, GE])
        hT = sb("hT", [P, GE])
        z = sb("z", [P, GE])
        xd = sb("xd", [P, 2 * GE])
        stats = sb("stats", [P, GT * 6])
        mv = sb("mv", [P, 2 * GT * 2])
        sc = sb("sc", [P, 2 * GT * 2])
        eps = sb("eps", [P, 1])
        junk = root_s[:, 0:GT * GE]

        psT, psR, psZ = (ps(n) for n in ("psT", "psR", "psZ"))
        psS = psZ
        psU = [[ps("psU00"), ps("psU01")], [ps("psU10"), ps("psU11")]]

        def sums(q, b, rows=P):
            return psU[q][b % 2][0:rows, (b // 2) * P:(b // 2 + 1) * P]

        def dram(name, shape, dt=f32):
            return nc.dram_tensor(name, shape, dt, kind="Internal").ap()

        node_tab = dram("node_tab", (N, 2))
        attr_d = dram("attr_d", (DE + 1, EP))
        rank3_d = dram("rank3_d", (3, EP))
        dis_d = dram("dis_d", (EP,))
        head_d = dram("head_d", (EP,))
        h_tab = [dram(f"h_tab{l}", (EP + 1, D)) for l in range(2)]
        v_tab = dram("v_tab", (EP + 1, D))
        out = t["out"]

        credits_ = sem("credits_")
        loaded = sem("loaded")
        zeroed = sem("zeroed")
        v_zeroed = sem("v_zeroed")
        dve_step = sem("dve_step")
        pool_step = sem("pool_step")
        seam_up = sem("seam_up")
        seam_flat = sem("seam_flat")
        seam_down = sem("seam_down")
        edge_ready = sem("edge_ready")
        edge_stored = sem("edge_stored")
        attr_loaded = sem("attr_loaded")
        attr_scaled = sem("attr_scaled")
        attr_stored = sem("attr_stored")
        turned_loaded = sem("turned_loaded")
        dis_turned = sem("dis_turned")
        tab_zeroed = [sem("tab_zeroed0"), sem("tab_zeroed1")]
        tab_free = [sem("tab_free0"), sem("tab_free1")]
        own_in = [sem("own_in0"), sem("own_in1")]
        own_kept = Count(sem("own_kept"))
        x_in = [sem("x_in0"), sem("x_in1")]
        x_based = Count(sem("x_based"))
        base_out = [sem("base_out0"), sem("base_out1")]
        dup_rows = [sem("dup_rows0"), sem("dup_rows1")]
        dup_done = Count(sem("dup_done"))
        idx_ready = sem("idx_ready")
        staged = sem("staged")
        gathered = [sem("gathered0"), sem("gathered1")]
        xd_in = [sem("xd_in0"), sem("xd_in1")]
        x1_out = [sem("x1_out0"), sem("x1_out1")]
        rows_in = [sem("rows_in0"), sem("rows_in1")]
        stored = [sem("stored0"), sem("stored1")]
        var_ready = sem("var_ready")
        root_ready = sem("root_ready")
        sum_var = Count(sem("sum_var"))
        sum_root = Count(sem("sum_root"))
        row_var = Count(sem("row_var"))
        row_root = Count(sem("row_root"))
        normed = Count(sem("normed"))
        g_ready = Count(sem("g_ready"))
        T_done = Count(sem("T_done"))
        hT_ready = Count(sem("hT_ready"))
        R_done = Count(sem("R_done"))
        rT_ready = Count(sem("rT_ready"))
        Z_done = Count(sem("Z_done"))
        z_ready = Count(sem("z_ready"))
        eq_ready = Count(sem("eq_ready"))
        U_done = Count(sem("U_done"), GT)
        carried = Count(sem("carried"), GT)
        stat_done = Count(sem("stat_done"), GT)
        U_free = Count(sem("U_free"))
        y_ready = Count(sem("y_ready"))
        act_done = Count(sem("act_done"))
        h_ready = Count(sem("h_ready"))
        x1_ready = Count(sem("x1_ready"))
        zz_ready = Count(sem("zz_ready"))
        T2_done = Count(sem("T2_done"))
        zT_ready = Count(sem("zT_ready"))
        V_done = Count(sem("V_done"))
        firsts_in = sem("firsts_in")
        firsts_out = sem("firsts_out")
        added = sem("added")
        v_loaded = [sem("v_loaded0"), sem("v_loaded1")]
        eqs_ready = Count(sem("eqs_ready"))
        M_done = Count(sem("M_done"))
        m_ready = Count(sem("m_ready"))
        C_done = Count(sem("C_done"))
        c_ready = Count(sem("c_ready"))

        def G(l, i, q):
            return i * 2 + (GROUPS * l + q)

        def cut(buf, q, b, w=P):
            return buf[:, (q * GT + b) * w:(q * GT + b + 1) * w]

        def part(buf, q, w=GE):
            return buf[:, q * w:(q + 1) * w]

        block = ctx.enter_context(nc.Block())

        @block.sync
        def _(sp):
            def load(dst, src):
                sp.dma_start(dst, src).then_inc(loaded, 16)

            load(dst_b[:, :], t["dst_b"])
            load(dst_b_prev[:, :], t["dst_b_prev"])
            load(dst_b_next[:, :], t["dst_b_next"])
            for k in range(3):
                load(pos_b[:, k * TILES:(k + 1) * TILES], t["pos_b"][k])
            load(ident[:, :], t["ident"])
            load(src_a[:, :], t["src_a"])
            load(dst_a[:, :], t["dst_a"])
            load(dst_a_prev[:, :], t["dst_a_prev"])
            load(dump_a[:, :], t["dump_a"])
            load(ew_a[:, :], t["ew_a"])
            load(before[:, :], t["before"])
            load(lin_w[:, :].rearrange("p (l d) -> p l d", l=LAYERS), t["lin_w"].rearrange("l p d -> p l d"))
            load(edge_w2[:, :].rearrange("p (l d) -> p l d", l=LAYERS), t["edge_w2"].rearrange("l p d -> p l d"))
            load(edge_w1[:, :].rearrange("p (l d) -> p l d", l=LAYERS), t["edge_w1"].rearrange("l p d -> p l d"))
            load(out_w[:, :], t["out_w"])
            load(ln_w[:, :], t["ln_w"].rearrange("(o l) d -> o (l d)", o=1).broadcast_to([P, LAYERS * D]))
            load(ln_b[:, :], t["ln_b"].rearrange("(o l) d -> o (l d)", o=1).broadcast_to([P, LAYERS * D]))
            load(last_bias[:, :], t["bias"][LAYERS - 1:LAYERS, :].broadcast_to([P, D]))
            load(carry[1:2, :], t["bias"].rearrange("(o l) d -> o (l d)", o=1))
            load(carry[2:3, :], t["edge_b2"].rearrange("(o l) d -> o (l d)", o=1))
            sp.dma_start(attr_s[:, :], t["attr_t"].rearrange("j (c r) -> (j c) r", c=8)).then_inc(attr_loaded, 16)

            sp.wait_ge(zeroed, 1)
            half = N // 2
            for q in range(2):
                sp.dma_start(node_tab[q * half:(q + 1) * half, :].rearrange("(p r) c -> p (r c)", p=50),
                             zeros[0:50, 0:2000]).then_inc(tab_zeroed[q], 16)
            for l in range(2):
                sp.dma_start(h_tab[l][0:1, :], zeros[0:1, 0:D]).then_inc(stored[l], 16)

            sp.dma_start(v_tab[0:1, :], zeros[0:1, 0:D]).then_inc(v_zeroed, 16)

            sp.wait_ge(edge_ready, 1)
            for dst, src in ((rank3_d[0], goes_on_b), (rank3_d[1], bias_row_b), (rank3_d[2], b2_row_b),
                             (attr_d[DE], root_b), (dis_d, dis_b), (head_d, head_b)):
                sp.dma_start(dst.rearrange("(p c) -> p c", c=TILES), src[:, :]).then_inc(edge_stored, 16)
            sp.wait_ge(edge_stored, 16 * 6)
            for j in range(DE):
                sp.dma_start(root_s[j * 8:(j + 1) * 8, :],
                             attr_d[DE].rearrange("(c r) -> c r", c=8)).then_inc(attr_loaded, 16)
            sp.dma_start(dis_t[:, :].rearrange("t (j p) -> t j p", j=GT),
                         dis_d.rearrange("(j t p) -> t j p", j=GT, p=P)).then_inc(turned_loaded, 16)
            with nc.allow_non_contiguous_dma(reason="one head row for each tile"):
                for j in range(GT):
                    sp.dma_start(first_head[:, j:j + 1],
                                 head_d.rearrange("(j t p) -> j t p", j=GT, p=P)[j, :, 0:1]).then_inc(turned_loaded, 16)

            xv = t["x"][0:P * RP, :].rearrange("(p r) d -> p (r d)", p=P)
            ov = out[0:P * RP, :].rearrange("(p r) d -> p (r d)", p=P)
            with sp.Fori(0, CHUNKS // 2) as i:
                for q in range(2):
                    sp.wait_ge(x_based.sem, x_based.free(i * 2 + q))
                    sp.dma_start(part(xin, q, CW), xv[:, bass.ds((i * 2 + q) * CW, CW)]).then_inc(x_in[q], 16)
                for q in range(2):
                    sp.wait_ge(x_based.sem, x_based.done(i * 2 + q))
                    sp.dma_start(ov[:, bass.ds((i * 2 + q) * CW, CW)], part(xout, q, CW)).then_inc(base_out[q], 16)
            sp.wait_ge(x_based.sem, x_based.free(CHUNKS))
            rest_in = xin[0:REST // 5, 0:5 * D]
            sp.dma_start(rest_in, t["x"][P * RP:N, :].rearrange("(p r) d -> p (r d)", r=5)).then_inc(x_in[0], 16)
            sp.wait_ge(x_based.sem, x_based.done(CHUNKS))
            sp.dma_start(out[P * RP:N, :].rearrange("(p r) d -> p (r d)", r=5),
                         xout[0:REST // 5, 0:5 * D]).then_inc(edge_stored, 16)
            sp.dma_start(out[DUMP:ROWS_OUT, :].rearrange("(p r) d -> p (r d)", p=P),
                         zeros[:, 0:GT * D]).then_inc(edge_stored, 16)
            sp.dma_start(out[N:N + 1, :], zeros[0:1, 0:D]).then_inc(edge_stored, 16)

            with sp.Fori(0, ITERS) as i:
                for q in range(2):
                    sp.wait_ge(dup_done.sem, dup_done.free(i * 2 + q))
                    sp.dma_start(part(rows_src, q), t["src_row"][0:1, bass.ds((i * 2 + q) * GE, GE)]
                                 .broadcast_to([P, GE])).then_inc(dup_rows[q], 16)
            sp.wait_ge(attr_scaled, 1)
            sp.dma_start(attr_d[0:DE].rearrange("j (c r) -> (j c) r", c=8), attr_s[:, :]).then_inc(attr_stored, 16)
            sp.wait_ge(attr_stored, 16)

            for l in range(LAYERS):
                with sp.Fori(0, ITERS) as i:
                    for q in range(2):
                        at = i * (-2 * GE) + (GROUPS - 1 - q) * GE
                        n = G(l, i, q)
                        sp.wait_ge(eq_ready.sem, eq_ready.free(n))
                        sp.wait_ge(U_done.sem, U_done.free(n))
                        sp.dma_start(part(rows, q), t["dst_row"][0:1, bass.ds(at, GE)]
                                     .broadcast_to([P, GE])).then_inc(rows_in[q], 16)
                        sp.dma_start(part(attr, q), attr_d[:, bass.ds(at, GE)]).then_inc(rows_in[q], 16)
                        sp.dma_start(part(rank3, q), rank3_d[:, bass.ds(at, GE)]).then_inc(rows_in[q], 16)

            sp.wait_ge(firsts_in, 16 * GT)
            for j in range(GT):
                sp.dma_start(v_tab[1:EP + 1, :].rearrange("(j t p) d -> j t p d", j=GT, p=P)[j, :, 0, :],
                             first_v[:, j * D:(j + 1) * D]).then_inc(firsts_out, 16)
            sp.wait_ge(firsts_out, 16 * GT)
            with sp.Fori(0, ITERS) as i:
                for q in range(2):
                    n = i * 2 + q
                    at = n * GE
                    sp.wait_ge(eqs_ready.sem, eqs_ready.free(n))
                    sp.wait_ge(M_done.sem, M_done.free(n))
                    sp.dma_start(part(rows, q), t["dst_row"][0:1, bass.ds(at, GE)]
                                 .broadcast_to([P, GE])).then_inc(v_loaded[q], 16)
                    sp.dma_start(part(rows_src, q), t["src_row"][0:1, bass.ds(at, GE)]
                                 .broadcast_to([P, GE])).then_inc(v_loaded[q], 16)
                    sp.dma_start(part(v_in, q).rearrange("p (b d) -> p b d", b=GT),
                                 v_tab[1:EP + 1, :].rearrange("(n p) d -> p n d", p=P)[:, bass.ds(n * GT, GT), :]
                                 ).then_inc(v_loaded[q], 16)

        @block.gpsimd
        def _(pool):
            steps = [0]

            def hold(s, value):
                if isinstance(value, int):
                    pool.wait_ge(s, value)
                    return
                r = pool.to_reg(value)
                pool.wait_ge(credits_, 1)
                pool.wait_ge(s, r)

            def peeled(body):
                body(0, True)
                with pool.Fori(1, ITERS) as i:
                    body(i, False)

            pool.memset(zeros[:, :], 0.0).then_inc(zeroed, 1)
            pool.memset(gat[:, :], 0.0)
            pool.memset(xd[:, :], 0.0)
            pool.memset(stage_row[:, :], 0.0)
            pool.memset(own[:, :], 0.0)
            pool.memset(carry[0:1, :], 0.0).then_inc(pool_step, 1)
            node_bound = pool.to_reg(N - 1)
            tab_bound = pool.to_reg(EP)
            out_bound = pool.to_reg(ROWS_OUT - 1)
            pool.wait_ge(pool_step, 1)

            pool.wait_ge(edge_ready, 1)
            for q in range(2):
                pool.wait_ge(tab_zeroed[q], 16)

            def fill_node_tab(i, first):
                for q in range(2):
                    if not first:
                        hold(tab_free[q], i * (16 * GT))
                    pool.tensor_copy(part(stage_idx, q, GT), node_idx_b[:, bass.ds((i * 2 + q) * GT, GT)])
                    pool.tensor_copy(part(stage_row, q, 2 * GT),
                                     node_row_b[:, bass.ds((i * 2 + q) * (2 * GT), 2 * GT)]).then_inc(staged, 1)
                    hold(staged, i * 2 + (q + 1))
                    for b in range(GT):
                        pool.indirect_dma_start(
                            node_tab[:, :], bass.IndirectOffsetOnAxis(ap=cut(stage_idx, q, b, 1), axis=0),
                            cut(stage_row, q, b, 2), None, bounds_check=node_bound,
                            oob_is_err=False).then_inc(tab_free[q], 16)

            peeled(fill_node_tab)
            for q in range(2):
                pool.wait_ge(tab_free[q], 16 * GT * ITERS)

            with pool.Fori(0, ITERS) as i:
                for q in range(2):
                    hold(own_kept.sem, own_kept.free(i * 2 + q))
                    pool.tensor_copy(part(stage_idx, q, GT),
                                     src_a[:, bass.ds((i * 2 + q) * GT, GT)]).then_inc(staged, 1)
                    hold(staged, i * 2 + (2 * ITERS + q + 1))
                    for b in range(GT):
                        pool.indirect_dma_start(
                            cut(stage_row, q, b, 2), None, node_tab[:, :],
                            bass.IndirectOffsetOnAxis(ap=cut(stage_idx, q, b, 1), axis=0),
                            bounds_check=node_bound, oob_is_err=False).then_inc(own_in[q], 16)
            pool.wait_ge(own_kept.sem, own_kept.done(GROUPS - 1))
            pool.wait_ge(idx_ready, 1)
            steps[0] = 4 * ITERS

            for l in range(LAYERS):
                last = l == LAYERS - 1
                if l:
                    for q in range(2):
                        pool.wait_ge(stored[q], 16 + 16 * ITERS * l)
                if last:
                    for q in range(2):
                        pool.wait_ge(base_out[q], 16 * (CHUNKS // 2))
                    pool.wait_ge(edge_stored, 16 * 9)
                idx = src_a if l == 0 else src_row_idx
                table, bound = (t["x"], node_bound) if l == 0 else (h_tab[l - 1], tab_bound)

                def layer(i, first):
                    for q in range(2):
                        n = G(l, i, q)
                        at = i * (-2 * GT) + (GROUPS - 1 - q) * GT
                        hold(T_done.sem, T_done.free(n))
                        if last:
                            if not first:
                                hold(x1_out[q], i * (16 * GT))
                            pool.tensor_copy(part(stage_idx2, q, GT), dst_a[:, bass.ds(at, GT)])
                            pool.tensor_copy(part(stage_idx3, q, GT), x1_idx[:, bass.ds(at, GT)])
                        pool.tensor_copy(part(stage_idx, q, GT), idx[:, bass.ds(at, GT)]).then_inc(staged, 1)
                        hold(staged, i * 2 + (steps[0] + q + 1))
                        for b in reversed(range(GT)):
                            pool.indirect_dma_start(
                                cut(gat, q, b), None, table[:, :],
                                bass.IndirectOffsetOnAxis(ap=cut(stage_idx, q, b, 1), axis=0),
                                bounds_check=bound, oob_is_err=False).then_inc(gathered[q], 16)
                        if last:
                            for b in range(GT):
                                pool.indirect_dma_start(
                                    cut(xd, q, b), None, t["x"][:, :],
                                    bass.IndirectOffsetOnAxis(ap=cut(stage_idx2, q, b, 1), axis=0),
                                    bounds_check=node_bound, oob_is_err=False).then_inc(xd_in[q], 16)
                    if last:
                        for q in range(2):
                            hold(x1_ready.sem, x1_ready.done(i * 2 + q))
                            for b in range(GT):
                                pool.indirect_dma_start(
                                    out[:, :], bass.IndirectOffsetOnAxis(ap=cut(stage_idx3, q, b, 1), axis=0),
                                    cut(x1, q, b), None, bounds_check=node_bound,
                                    oob_is_err=False).then_inc(x1_out[q], 16)

                peeled(layer)
                steps[0] += 2 * ITERS

            for q in range(2):
                pool.wait_ge(stored[q], 16 + 16 * ITERS * LAYERS)
                pool.wait_ge(x1_out[q], 16 * GT * ITERS)
            pool.wait_ge(v_zeroed, 16)
            for j in range(GT):
                pool.indirect_dma_start(
                    first_v[:, j * D:(j + 1) * D], None, v_tab[:, :],
                    bass.IndirectOffsetOnAxis(ap=first_idx[:, j:j + 1], axis=0),
                    bounds_check=tab_bound, oob_is_err=False).then_inc(firsts_in, 16)

            def add_messages(i, first):
                for q in range(2):
                    n = i * 2 + q
                    hold(c_ready.sem, c_ready.done(n))
                    if q or not first:
                        hold(added, n * (16 * GT))
                    pool.tensor_copy(part(stage_idx, 0, GT), add_idx[:, bass.ds(n * GT, GT)]).then_inc(staged, 1)
                    hold(staged, n + (steps[0] + 1))
                    for b in range(GT):
                        pool.indirect_dma_start(
                            out[:, :], bass.IndirectOffsetOnAxis(ap=cut(stage_idx, 0, b, 1), axis=0),
                            cut(ho, q, b), None, bounds_check=out_bound,
                            oob_is_err=True, compute_op=ALU.add).then_inc(added, 16)

            peeled(add_messages)
            pool.wait_ge(added, 16 * GT * GROUPS)

        @block.vector
        def _(dve):
            v = nc.vector
            chain = [0]

            def link(ins):
                chain[0] += 1
                ins.then_inc(dve_step, 1)
                dve.wait_ge(dve_step, chain[0])

            for c in (sum_var, sum_root, row_var, row_root, own_kept, x_based, dup_done, normed, g_ready, T_done, hT_ready, R_done, rT_ready,
                      Z_done, z_ready, eq_ready, U_done, carried, stat_done, U_free, y_ready, act_done, h_ready,
                      x1_ready, zz_ready, T2_done, zT_ready, V_done, eqs_ready, M_done, m_ready, C_done,
                      c_ready):
                dve.sem_inc(c.sem, c.credit)
            dve.sem_inc(credits_, 1)
            v.memset(eps[:, :], LN_EPS)

            dve.wait_ge(loaded, 16 * 22)
            pos1, tile0, tile1 = (pos_b[:, k * TILES:(k + 1) * TILES] for k in range(3))
            v.tensor_tensor(is_head_b[:, :], dst_b[:, :], dst_b_prev[:, :], ALU.not_equal)
            link(v.tensor_tensor(is_tail_b[:, :], dst_b[:, :], dst_b_next[:, :], ALU.not_equal))
            v.tensor_tensor(tmp_b[:, :], is_head_b[:, :], pos1, ALU.mult)
            link(v.scalar_tensor_tensor(tail_b[:, :], pos1, -FAR, is_tail_b[:, :], ALU.add, ALU.mult))
            link(v.tensor_scalar(tail_b[:, :], tail_b[:, :], FAR, None, ALU.add))
            v.tensor_tensor_scan(head_b[:, :], tmp_b[:, :], tmp_b[:, :], 0.0, ALU.max, ALU.max)
            link(v.tensor_tensor_scan(tail_b[:, ::-1], tail_b[:, ::-1], tail_b[:, ::-1], FAR, ALU.min, ALU.min))
            v.tensor_copy(seam[:, 0:1], head_b[:, TILES - 1:TILES])
            v.tensor_copy(seam[:, 1:2], tail_b[:, 0:1]).then_inc(seam_up, 1)
            dve.wait_ge(seam_flat, 1)
            v.tensor_copy(seam_row[0:1, 0:P], psS[0:1, 0:P])
            link(v.tensor_copy(seam_row[0:1, P:2 * P], psS[0:1, P:2 * P]))
            v.memset(seam_row[0:1, 2 * P:2 * P + 1], 0.0)
            v.memset(seam_row[0:1, 4 * P - 1:4 * P], FAR)
            v.tensor_tensor_scan(seam_row[0:1, 2 * P + 1:3 * P], seam_row[0:1, 0:P - 1], seam_row[0:1, 0:P - 1],
                                 0.0, ALU.max, ALU.max)
            v.tensor_tensor_scan(seam_row[0:1, 3 * P:4 * P - 1][:, ::-1], seam_row[0:1, P + 1:2 * P][:, ::-1],
                                 seam_row[0:1, P + 1:2 * P][:, ::-1], FAR, ALU.min, ALU.min).then_inc(seam_up, 1)
            dve.wait_ge(seam_down, 1)
            link(v.tensor_copy(seam[:, 2:4], psS[:, 2 * P:2 * P + 2]))
            v.tensor_scalar(head_b[:, :], head_b[:, :], seam[:, 2:3], None, ALU.max)
            link(v.tensor_scalar(tail_b[:, :], tail_b[:, :], seam[:, 3:4], None, ALU.min))
            link(v.scalar_tensor_tensor(deg_b[:, :], tail_b[:, :], 1.0, head_b[:, :], ALU.add, ALU.subtract))
            v.engine_nop().then_inc(var_ready, 1)
            dve.wait_ge(root_ready, 1)
            link(v.reciprocal(dis_b[:, :], root_b[:, :]))
            v.tensor_tensor(goes_on_b[:, :], tail_b[:, :], tile1, ALU.is_gt)
            v.tensor_tensor(tmp_b[:, :], head_b[:, :], tile0, ALU.max)
            link(v.tensor_tensor(b2_row_b[:, :], tail_b[:, :], tile1, ALU.min))
            link(v.scalar_tensor_tensor(b2_row_b[:, :], b2_row_b[:, :], 1.0, tmp_b[:, :], ALU.add, ALU.subtract))
            v.tensor_tensor(b2_row_b[:, :], b2_row_b[:, :], root_b[:, :], ALU.mult)
            link(v.tensor_scalar(bias_row_b[:, :], goes_on_b[:, :], -1.0, 1.0, ALU.mult, ALU.add))
            v.tensor_tensor(bias_row_b[:, :], bias_row_b[:, :], root_b[:, :], ALU.mult)
            row2 = node_row_b[:, :].rearrange("p (c k) -> p c k", k=2)
            v.tensor_copy(row2[:, :, 0], pos1)
            v.tensor_copy(row2[:, :, 1], deg_b[:, :])
            link(v.scalar_tensor_tensor(tmp_b[:, :], dst_b[:, :], -float(SKIP), is_head_b[:, :], ALU.add, ALU.mult))
            v.tensor_scalar(node_idx_b[:, :], tmp_b[:, :], float(SKIP), None, ALU.add).then_inc(edge_ready, 1)

            cc = cols[:, :].rearrange("p (c k) -> p c k", k=4)
            co = cols_out[:, :].rearrange("p (c k) -> p c k", k=4)
            v.tensor_copy(cc[:, :, 0], dst_a[:, :])
            v.tensor_copy(co[:, :, 0], dst_a[:, :])
            v.tensor_copy(co[:, :, 2], src_a[:, :])
            v.tensor_copy(src_f[:, :], src_a[:, :])
            v.tensor_copy(co[:, :, 3], ew_a[:, :])
            link(v.tensor_tensor(is_head_a[:, :], dst_a[:, :], dst_a_prev[:, :], ALU.not_equal))
            link(v.tensor_copy(co[:, :, 1], is_head_a[:, :]))
            v.memset(co[0:1, :, 1], 1.0)
            link(v.scalar_tensor_tensor(tmp_a[:, :], dst_a[:, :], -float(SKIP), is_head_a[:, :], ALU.add, ALU.mult))
            link(v.tensor_scalar(x1_idx[:, :], tmp_a[:, :], float(SKIP), None, ALU.add))
            dve.wait_ge(turned_loaded, 16 * (GT + 1))
            v.tensor_copy(first_idx[:, :], first_head[:, :])
            dve.wait_ge(dis_turned, 1)
            link(v.tensor_copy(cc[:, :, 1], psR[:, 0:TILES]))
            v.tensor_tensor(cc[:, :, 2], cc[:, :, 1], cc[:, :, 1], ALU.mult)
            dve.wait_ge(attr_loaded, 16 * (DE + 1))
            v.tensor_tensor(attr_s[:, :], attr_s[:, :], root_s[:, :], ALU.mult).then_inc(attr_scaled, 1)

            L2 = slice((LAYERS - 1) * D, LAYERS * D)
            link(v.bn_stats(stats[:, 0:6], last_bias[:, :]))
            link(v.bn_aggr(mv[:, 0:2], stats[:, 0:6]))
            v.engine_nop().then_inc(var_ready, 1)
            dve.wait_ge(root_ready, 2)
            link(v.reciprocal(sc[:, 0:1], sc[:, 2:3]))
            link(v.scalar_tensor_tensor(base[:, :], last_bias[:, :], mv[:, 0:1], ln_w[:, L2], ALU.subtract, ALU.mult))
            link(v.scalar_tensor_tensor(base[:, :], base[:, :], sc[:, 0:1], ln_b[:, L2], ALU.mult, ALU.add))
            link(v.tensor_scalar(base[:, :], base[:, :], 0.0, None, ALU.max))

            def add_base(q, parts, n):
                xi = xin[0:parts, q * CW:q * CW + n * D].rearrange("p (r d) -> p r d", d=D)
                xo = xout[0:parts, q * CW:q * CW + n * D].rearrange("p (r d) -> p r d", d=D)
                bb = base[0:parts, :].rearrange("p (o d) -> p o d", o=1).broadcast_to([parts, n, D])
                return v.tensor_tensor(xo, xi, bb, ALU.add)

            for q in range(2):
                dve.wait_ge(x_in[q], 16)
                add_base(q, P, CR).then_inc(x_based.sem, 1)
            with dve.Fori(1, CHUNKS // 2) as i:
                for q in range(2):
                    dve.wait_ge(x_in[q], i * 16 + 16)
                    dve.wait_ge(base_out[q], i * 16)
                    add_base(q, P, CR).then_inc(x_based.sem, 1)
            dve.wait_ge(x_in[0], 16 * (CHUNKS // 2 + 1))
            dve.wait_ge(base_out[0], 16 * (CHUNKS // 2))
            add_base(0, REST // 5, 5).then_inc(x_based.sem, 1)

            with dve.Fori(0, ITERS) as i:
                for q in range(2):
                    n = i * 2 + q
                    dve.wait_ge(dup_rows[q], i * 16 + 16)
                    dve.wait_ge(dup_done.sem, dup_done.done(n) - 1)
                    for b in range(GT):
                        ins = v.scalar_tensor_tensor(
                            junk[:, b * GE:(b + 1) * GE], part(rows_src, q), src_f[:, bass.ds(n * GT + b, 1)],
                            before[:, b * GE:(b + 1) * GE], ALU.is_equal, ALU.mult,
                            accum_out=earlier[:, bass.ds(n * GT + b, 1)])
                    ins.then_inc(dup_done.sem, 1)
            dve.wait_ge(dup_done.sem, dup_done.done(GROUPS - 1))
            v.tensor_tensor(tmp_a[:, :], src_f[:, :], dump_a[:, :], ALU.subtract)
            link(v.tensor_scalar(earlier[:, :], earlier[:, :], 0.0, None, ALU.is_equal))
            link(v.tensor_tensor(tmp_a[:, :], tmp_a[:, :], earlier[:, :], ALU.mult))
            link(v.tensor_tensor(add_idx[:, :], tmp_a[:, :], dump_a[:, :], ALU.add))
            dve.wait_ge(own_kept.sem, own_kept.done(GROUPS - 1))
            ow = own[:, :].rearrange("p (c k) -> p c k", k=2)
            v.tensor_copy(src_row_idx[:, :], ow[:, :, 0])
            v.tensor_scalar(earlier[:, :], ow[:, :, 1], 0.0, None, ALU.is_gt)
            v.tensor_scalar(tmp_a[:, :], ow[:, :, 1], 1e-30, None, ALU.max).then_inc(var_ready, 1)
            dve.wait_ge(root_ready, 3)
            link(v.reciprocal(tmp_a[:, :], tmp_a[:, :]))
            link(v.tensor_tensor(cc[:, :, 3], tmp_a[:, :], earlier[:, :], ALU.mult))
            v.engine_nop().then_inc(idx_ready, 1)

            for l in range(LAYERS):
                first, last = l == 0, l == LAYERS - 1
                LW = slice(l * D, (l + 1) * D)
                K = 6 if first or last else 3
                start = chain[0]
                with dve.Fori(0, ITERS) as i:
                    for q in range(2):
                        n = G(l, i, q)
                        k = [0]

                        def step(ins, alone=False):
                            k[0] += 1
                            ins.then_inc(dve_step, 1)
                            value = i * (2 * K) + (start + q * K + k[0])
                            if alone:
                                value = dve.to_reg(value)
                                dve.wait_ge(credits_, 1)
                            dve.wait_ge(dve_step, value)

                        def stc(c):
                            return part(stage_cols, q, 4 * GT).rearrange("p (b k) -> p b k", k=4)[:, :, c]

                        def col(buf, b, c, w):
                            return buf[:, q * w * GT + b * w + c:q * w * GT + b * w + c + 1]

                        m2 = part(mv, q, 2 * GT).rearrange("p (b k) -> p b k", k=2)
                        s2 = part(sc, q, 2 * GT).rearrange("p (b k) -> p b k", k=2)
                        dve.wait_ge(act_done.sem, act_done.free(n))
                        step(v.tensor_copy(part(stage_cols, q, 4 * GT),
                                           cols[:, bass.ds(i * (-8 * GT) + (GROUPS - 1 - q) * (4 * GT), 4 * GT)]))
                        if first:
                            dve.wait_ge(gathered[q], i * (16 * GT) + 16 * GT)
                            for b in range(GT):
                                ins = v.bn_stats(stats[:, 6 * b:6 * b + 6], cut(gat, q, b))
                            step(ins, alone=True)
                            for b in range(GT):
                                ins = v.bn_aggr(m2[:, b, :], stats[:, 6 * b:6 * b + 6])
                            ins.then_inc(row_var.sem, 1)
                            dve.wait_ge(row_root.sem, row_root.done(n))
                            step(v.reciprocal(s2[:, :, 0], s2[:, :, 0]))
                            step(v.tensor_tensor(s2[:, :, 0], s2[:, :, 0], stc(3), ALU.mult))
                            v.scalar_tensor_tensor(s2[:, :, 1], m2[:, :, 0], -1.0, s2[:, :, 0],
                                                   ALU.mult, ALU.mult).then_inc(normed.sem, 1)
                        dve.wait_ge(rows_in[q], i * 48 + (48 * (ITERS * l + 1)))
                        dve.wait_ge(U_done.sem, U_done.free(n))
                        for b in range(GT):
                            ins = v.tensor_scalar(cut(eq, q, b), cut(rows, q, b), col(stage_cols, b, 0, 4),
                                                  None, ALU.is_equal)
                        ins.then_inc(eq_ready.sem, 1)
                        if first:
                            dve.wait_ge(g_ready.sem, g_ready.done(n))
                        for s, b in enumerate(reversed(range(GT))):
                            dve.wait_ge(U_done.sem, U_done.done(n, s + 1))
                            v.tensor_copy(carry[0:1, LW], sums(q, b, 1)).then_inc(carried.sem, 1)
                            ins = v.bn_stats(stats[:, 6 * b:6 * b + 6], sums(q, b))
                            ins.then_inc(stat_done.sem, 1)
                        all_stats = dve.to_reg(stat_done.done(n))
                        dve.wait_ge(credits_, 1)
                        dve.wait_ge(stat_done.sem, all_stats)
                        for b in range(GT):
                            ins = v.bn_aggr(m2[:, b, :], stats[:, 6 * b:6 * b + 6])
                        step(ins)
                        v.tensor_tensor(s2[:, :, 0], m2[:, :, 1], stc(2), ALU.mult).then_inc(sum_var.sem, 1)
                        dve.wait_ge(sum_root.sem, sum_root.done(n))
                        step(v.reciprocal(s2[:, :, 0], s2[:, :, 0]))
                        v.tensor_tensor(s2[:, :, 0], s2[:, :, 0], stc(1), ALU.mult)
                        for b in range(GT):
                            ins = v.scalar_tensor_tensor(cut(y, q, b), sums(q, b),
                                                         col(mv, b, 0, 2), ln_w[:, LW], ALU.subtract, ALU.mult)
                        ins.then_inc(U_free.sem, 1)
                        dve.wait_ge(U_free.sem, U_free.done(n))
                        for b in range(GT):
                            ins = v.scalar_tensor_tensor(cut(y, q, b), cut(y, q, b), col(sc, b, 0, 2),
                                                         ln_b[:, LW], ALU.mult, ALU.add)
                        ins.then_inc(y_ready.sem, 1)
                        if last:
                            m = i * 2 + q
                            dve.wait_ge(h_ready.sem, h_ready.done(m))
                            dve.wait_ge(xd_in[q], i * (16 * GT) + 16 * GT)
                            step(v.tensor_tensor(part(x1, q), part(xd, q), part(y, q), ALU.add))
                            for b in range(GT):
                                ins = v.bn_stats(stats[:, 6 * b:6 * b + 6], cut(x1, q, b))
                            step(ins, alone=True)
                            for b in range(GT):
                                ins = v.bn_aggr(m2[:, b, :], stats[:, 6 * b:6 * b + 6])
                            ins.then_inc(row_var.sem, 1)
                            dve.wait_ge(row_root.sem, row_root.done(m + GROUPS))
                            step(v.reciprocal(s2[:, :, 0], s2[:, :, 0]))
                            v.scalar_tensor_tensor(s2[:, :, 1], m2[:, :, 0], -1.0, s2[:, :, 0],
                                                   ALU.mult, ALU.mult).then_inc(x1_ready.sem, 1)
                        assert k[0] == K, (l, k[0])
                chain[0] += K * 2 * ITERS

            start = chain[0]
            with dve.Fori(0, ITERS) as i:
                for q in range(2):
                    n = i * 2 + q
                    dve.wait_ge(m_ready.sem, m_ready.free(n))
                    v.tensor_copy(part(stage_cols, q, 4 * GT),
                                  cols_out[:, bass.ds(n * (4 * GT), 4 * GT)]).then_inc(dve_step, 1)
                    dve.wait_ge(dve_step, n + (start + 1))
                    dve.wait_ge(v_loaded[q], i * 48 + 48)
                    dve.wait_ge(C_done.sem, C_done.free(n))
                    for b in range(GT):
                        c0 = (q * GT + b) * 4
                        v.tensor_scalar(cut(eq, q, b), cut(rows, q, b), stage_cols[:, c0:c0 + 1],
                                        stage_cols[:, c0 + 1:c0 + 2], ALU.is_equal, ALU.mult)
                        ins = v.tensor_scalar(cut(same_src, q, b, GE), part(rows_src, q),
                                              stage_cols[:, c0 + 2:c0 + 3], None, ALU.is_equal)
                    ins.then_inc(eqs_ready.sem, 1)

        @block.scalar
        def _(act):
            a = nc.scalar
            act.wait_ge(credits_, 1)
            act.wait_ge(pool_step, 1)
            act.wait_ge(var_ready, 1)
            a.activation(root_b[:, :], deg_b[:, :], ACT.Sqrt).then_inc(root_ready, 1)
            act.wait_ge(var_ready, 2)
            a.activation(sc[:, 2:3], mv[:, 1:2], ACT.Sqrt, bias=eps[:, :]).then_inc(root_ready, 1)
            with act.Fori(0, ITERS) as i:
                for q in range(2):
                    act.wait_ge(own_in[q], i * (16 * GT) + 16 * GT)
                    a.copy(own[:, bass.ds((i * 2 + q) * (2 * GT), 2 * GT)],
                           part(stage_row, q, 2 * GT)).then_inc(own_kept.sem, 1)

            act.wait_ge(var_ready, 3)
            a.activation(tmp_a[:, :], tmp_a[:, :], ACT.Sqrt).then_inc(root_ready, 1)

            def roots(done, var, q):
                s = part(sc, q, 2 * GT).rearrange("p (b k) -> p b k", k=2)[:, :, 0]
                a.activation(s, var, ACT.Sqrt, bias=eps[:, :]).then_inc(done.sem, 1)

            for l in range(LAYERS):
                first, last = l == 0, l == LAYERS - 1
                table = v_tab if last else h_tab[l]
                with act.Fori(0, ITERS) as i:
                    for q in range(2):
                        n = G(l, i, q)
                        m = i * 2 + q
                        if first:
                            act.wait_ge(row_var.sem, row_var.done(n))
                            roots(row_root, part(mv, q, 2 * GT).rearrange("p (b k) -> p b k", k=2)[:, :, 1], q)
                            act.wait_ge(normed.sem, normed.done(n))
                            for b in range(GT):
                                c = (q * GT + b) * 2
                                ins = a.activation(cut(gat, q, b), cut(gat, q, b), ACT.Relu,
                                                   bias=sc[:, c + 1:c + 2], scale=sc[:, c:c + 1])
                            ins.then_inc(g_ready.sem, 1)
                        act.wait_ge(T_done.sem, T_done.done(n))
                        a.copy(hT[:, :], psT[:, :]).then_inc(hT_ready.sem, 1)
                        act.wait_ge(R_done.sem, R_done.done(n))
                        a.activation(rT[:, :], psR[:, :], ACT.Relu).then_inc(rT_ready.sem, 1)
                        act.wait_ge(Z_done.sem, Z_done.done(n))
                        a.copy(z[:, :], psZ[:, :]).then_inc(z_ready.sem, 1)
                        act.wait_ge(sum_var.sem, sum_var.done(n))
                        roots(sum_root, part(sc, q, 2 * GT).rearrange("p (b k) -> p b k", k=2)[:, :, 0], q)
                        act.wait_ge(y_ready.sem, y_ready.done(n))
                        act.wait_ge(stored[q], i * 16 + (16 + 16 * ITERS * l))
                        if not last:
                            for b in range(GT):
                                c = (q * GT + b) * 4
                                ins = a.activation(cut(ho, q, b), cut(y, q, b), ACT.Relu,
                                                   scale=stage_cols[:, c + 1:c + 2])
                            ins.then_inc(act_done.sem, 1)
                            act.wait_ge(act_done.sem, act_done.done(n))
                        else:
                            a.activation(part(y, q), part(y, q), ACT.Relu).then_inc(h_ready.sem, 1)
                            act.wait_ge(row_var.sem, row_var.done(m + GROUPS))
                            roots(row_root, part(mv, q, 2 * GT).rearrange("p (b k) -> p b k", k=2)[:, :, 1], q)
                            act.wait_ge(x1_ready.sem, x1_ready.done(m))
                            for b in range(GT):
                                c = (q * GT + b) * 2
                                ins = a.activation(zz[:, b * P:(b + 1) * P], cut(x1, q, b), ACT.Relu,
                                                   bias=sc[:, c + 1:c + 2], scale=sc[:, c:c + 1])
                            ins.then_inc(zz_ready.sem, 1)
                            act.wait_ge(T2_done.sem, T2_done.done(m))
                            a.copy(hT[:, :], psT[:, :]).then_inc(zT_ready.sem, 1)
                            act.wait_ge(V_done.sem, V_done.done(m))
                            a.copy(part(ho, q), psR[:, :]).then_inc(act_done.sem, 1)
                            act.wait_ge(act_done.sem, act_done.done(n))
                        act.dma_start(
                            table[1:EP + 1, :].rearrange("(c p) d -> p c d", p=P)[
                                :, bass.ds(i * (-2 * GT) + (GROUPS - 1 - q) * GT, GT), :],
                            part(ho, q).rearrange("p (b d) -> p b d", b=GT)).then_inc(stored[q], 16)

            for q in range(2):
                act.wait_ge(stored[q], 16 + 16 * ITERS * LAYERS)
            with act.Fori(0, ITERS) as i:
                for q in range(2):
                    n = i * 2 + q
                    act.wait_ge(M_done.sem, M_done.done(n))
                    for b in range(GT):
                        c = (q * GT + b) * 4 + 3
                        ins = a.activation(z[:, b * P:(b + 1) * P], psZ[:, b * P:(b + 1) * P], ACT.Copy,
                                           scale=stage_cols[:, c:c + 1])
                    ins.then_inc(m_ready.sem, 1)
                    act.wait_ge(C_done.sem, C_done.done(n))
                    act.wait_ge(staged, n + 2 * ITERS * (2 + LAYERS))
                    a.copy(part(ho, q), psT[:, :]).then_inc(c_ready.sem, 1)

        @block.tensor
        def _(pe):
            T = nc.tensor
            pe.wait_ge(credits_, 1)
            pe.wait_ge(loaded, 16 * 22)
            pe.wait_ge(seam_up, 1)
            T.transpose(psS[0:1, 0:P], seam[:, 0:1], ident[:, :])
            T.transpose(psS[0:1, P:2 * P], seam[:, 1:2], ident[:, :]).then_inc(seam_flat, 1)
            pe.wait_ge(seam_up, 2)
            T.matmul(psS[:, 2 * P:2 * P + 1], seam_row[0:1, 2 * P:3 * P], ident[0:1, 0:1], start=True, stop=True)
            T.matmul(psS[:, 2 * P + 1:2 * P + 2], seam_row[0:1, 3 * P:4 * P], ident[0:1, 0:1],
                     start=True, stop=True).then_inc(seam_down, 1)
            pe.wait_ge(turned_loaded, 16 * (GT + 1))
            for j in range(GT):
                ins = T.transpose(psR[:, j * TQ:(j + 1) * TQ], dis_t[:, j * P:(j + 1) * P], ident[0:TQ, 0:TQ])
            ins.then_inc(dis_turned, 1)

            for l in range(LAYERS):
                first, last = l == 0, l == LAYERS - 1
                LW = slice(l * D, (l + 1) * D)
                if first:
                    pe.wait_ge(idx_ready, 1)
                with pe.Fori(0, ITERS) as i:
                    for q in range(2):
                        n = G(l, i, q)
                        m = i * 2 + q
                        if first:
                            pe.wait_ge(g_ready.sem, g_ready.done(n))
                        else:
                            pe.wait_ge(gathered[q], i * (16 * GT) + (16 * GT * (ITERS * l + 1)))
                        pe.wait_ge(hT_ready.sem, hT_ready.done(n) - 1)
                        if last:
                            pe.wait_ge(zT_ready.sem, zT_ready.done(m) - 1)
                        for b in range(GT):
                            ins = T.transpose(psT[:, b * P:(b + 1) * P], cut(gat, q, b), ident[:, :])
                        ins.then_inc(T_done.sem, 1)
                        pe.wait_ge(rows_in[q], i * 48 + (48 * (ITERS * l + 1)))
                        pe.wait_ge(rT_ready.sem, rT_ready.done(n) - 1)
                        if last:
                            pe.wait_ge(act_done.sem, act_done.done(n) - 1)
                        pe.wait_ge(credits_, 1)
                        T.matmul(psR[:, :], edge_w1[:, LW], part(attr, q), start=True, stop=True).then_inc(R_done.sem, 1)
                        pe.wait_ge(hT_ready.sem, hT_ready.done(n))
                        pe.wait_ge(rT_ready.sem, rT_ready.done(n))
                        pe.wait_ge(z_ready.sem, z_ready.done(n) - 1)
                        for b in range(GT):
                            zb = psZ[:, b * P:(b + 1) * P]
                            T.matmul(zb, hT[:, b * P:(b + 1) * P], lin_w[:, LW], start=True, stop=False)
                            ins = T.matmul(zb, rT[:, b * P:(b + 1) * P], edge_w2[:, LW], start=False, stop=True)
                        ins.then_inc(Z_done.sem, 1)
                        pe.wait_ge(z_ready.sem, z_ready.done(n))
                        pe.wait_ge(eq_ready.sem, eq_ready.done(n))
                        pe.wait_ge(U_free.sem, U_free.free(n))
                        for s, b in enumerate(reversed(range(GT))):
                            ub = sums(q, b)
                            if s >= 2:
                                pe.wait_ge(stat_done.sem, stat_done.done(n, s - 1))
                            T.matmul(ub, cut(eq, q, b), z[:, b * P:(b + 1) * P], start=True, stop=False)
                            pe.wait_ge(credits_, 1)
                            pe.wait_ge(carried.sem, carried.done(n, s))
                            T.matmul(ub, rank3[:, (q * GT + b) * P:(q * GT + b + 1) * P], carry[:, LW],
                                     start=False, stop=True).then_inc(U_done.sem, 1)
                        if last:
                            pe.wait_ge(zz_ready.sem, zz_ready.done(m))
                            for b in range(GT):
                                ins = T.transpose(psT[:, b * P:(b + 1) * P], zz[:, b * P:(b + 1) * P], ident[:, :])
                            ins.then_inc(T2_done.sem, 1)
                            pe.wait_ge(zT_ready.sem, zT_ready.done(m))
                            for b in range(GT):
                                ins = T.matmul(psR[:, b * P:(b + 1) * P], hT[:, b * P:(b + 1) * P], out_w[:, :],
                                               start=True, stop=True)
                            ins.then_inc(V_done.sem, 1)

            with pe.Fori(0, ITERS) as i:
                for q in range(2):
                    n = i * 2 + q
                    pe.wait_ge(v_loaded[q], i * 48 + 48)
                    pe.wait_ge(eqs_ready.sem, eqs_ready.done(n))
                    pe.wait_ge(m_ready.sem, m_ready.done(n) - 1)
                    for b in range(GT):
                        ins = T.matmul(psZ[:, b * P:(b + 1) * P], cut(eq, q, b), cut(v_in, q, b), start=True, stop=True)
                    ins.then_inc(M_done.sem, 1)
                    pe.wait_ge(m_ready.sem, m_ready.done(n))
                    pe.wait_ge(c_ready.sem, c_ready.done(n) - 1)
                    for b in range(GT):
                        for k in range(GT):
                            s0 = (q * GT + k) * GE + b * P
                            ins = T.matmul(psT[:, b * P:(b + 1) * P], same_src[:, s0:s0 + P],
                                           z[:, k * P:(k + 1) * P], start=(k == 0), stop=(k == GT - 1))
                    ins.then_inc(C_done.sem, 1)


def kernel(x, src, dst, edge_attr_16, edge_weight, L0_gnn_lin_w, L0_gnn_edge_w1, L0_gnn_edge_b1, L0_gnn_edge_w2,
           L0_gnn_edge_b2, L0_gnn_bias, L0_gnn_ln_w, L0_gnn_ln_b, L1_gnn_W):
    import numpy as np
    import concourse.bacc as bacc
    from concourse import mybir as mb
    from concourse.bass_utils import run_bass_kernel_spmd

    def padded(a, fill):
        return np.concatenate([a, np.full((EP - E,) + a.shape[1:], fill, a.dtype)])

    def lay_a(a):
        return np.ascontiguousarray(a.reshape(TILES, P).T)

    def lay_b(a):
        return np.ascontiguousarray(a.reshape(P, TILES))

    src, dst = (np.asarray(a) for a in (src, dst))
    src_p, dst_p = padded(src, N), padded(dst, N)
    none = np.full((1,), -1, dst.dtype)
    prev, after = np.concatenate([none, dst_p[:-1]]), np.concatenate([dst_p[1:], none])
    pos = np.arange(EP, dtype=np.float32)
    tile0 = np.arange(TILES, dtype=np.float32).repeat(P) * P
    c = np.arange(GE)
    before = (c[None, None, :] < (c.reshape(GT, P).T)[:, :, None]).astype(np.float32).reshape(P, GT * GE)
    arrays = {
        "x": np.ascontiguousarray(x),
        "src_a": lay_a(src_p), "dst_a": lay_a(dst_p), "dst_a_prev": lay_a(prev),
        "ew_a": lay_a(padded(np.asarray(edge_weight), 0.0)),
        "dump_a": lay_a(np.tile(np.arange(GE, dtype=np.float32) + DUMP, GROUPS)),
        "dst_b": lay_b(dst_p), "dst_b_prev": lay_b(prev), "dst_b_next": lay_b(after),
        "pos_b": np.stack([lay_b(pos + 1), lay_b(tile0 + 1), lay_b(tile0 + P)]),
        "dst_row": dst_p[None, :], "src_row": src_p[None, :],
        "attr_t": np.ascontiguousarray(padded(np.asarray(edge_attr_16), 0.0).T),
        "lin_w": np.ascontiguousarray(L0_gnn_lin_w), "edge_w2": np.ascontiguousarray(L0_gnn_edge_w2),
        "edge_w1": np.concatenate([np.asarray(L0_gnn_edge_w1), np.asarray(L0_gnn_edge_b1)[:, None, :]], axis=1),
        "edge_b2": np.ascontiguousarray(L0_gnn_edge_b2), "bias": np.ascontiguousarray(L0_gnn_bias),
        "ln_w": np.ascontiguousarray(L0_gnn_ln_w), "ln_b": np.ascontiguousarray(L0_gnn_ln_b),
        "out_w": np.ascontiguousarray(L1_gnn_W),
        "ident": np.eye(P, dtype=np.float32), "before": before,
    }
    nc = bacc.Bacc("TRN2", target_bir_lowering=False, num_devices=1)
    t = {k: nc.dram_tensor(f"in_{k}", a.shape, mb.dt.from_np(a.dtype), kind="ExternalInput").ap()
         for k, a in arrays.items()}
    t["out"] = nc.dram_tensor("out", (ROWS_OUT, D), mb.dt.float32, kind="ExternalOutput").ap()
    gnn(nc, t)
    r = run_bass_kernel_spmd(nc, [{f"in_{k}": a for k, a in arrays.items()}], core_ids=[0])
    return r.results[0]["out"][:N]
```

```python
import concourse.bass as bass
from concourse import mybir
from contextlib import ExitStack

N = 100000
E = 50000
D = 128
DE = 16
LAYERS = 3
P = 128
GT = 4
GROUPS = -(-E // (P * GT))
ITERS = GROUPS // 2
TILES = GROUPS * GT
EP = TILES * P
GE = GT * P
DUMP = N + 1
ROWS_OUT = DUMP + GE
SKIP = 2 * N
LN_EPS = 1e-5
FAR = 2.0 * EP
RP, CR = 780, 13
CHUNKS = RP // CR
REST = N - P * RP
CW = CR * D
TQ = TILES // GT
STAGED_BEFORE = GROUPS * (2 + LAYERS + 1) + 1


class Count:

    def __init__(self, sem, per=1, credit=None):
        self.sem, self.per = sem, per
        self.credit = 2 * per if credit is None else credit

    def done(self, n, k=None):
        return n * self.per + (self.credit + (self.per if k is None else k))

    def free(self, n):
        return n * self.per + (self.credit - self.per)


def gnn(nc, t):
    f32, i32 = mybir.dt.float32, mybir.dt.int32
    ALU, ACT = mybir.AluOpType, mybir.ActivationFunctionType
    ctx = ExitStack()
    with ctx:
        def sb(name, shape, dt=f32):
            return ctx.enter_context(nc.sbuf_tensor(name, shape, dt))

        def ps(name):
            return ctx.enter_context(nc.psum_tensor(name, [P, GE], f32))

        def sem(name):
            return ctx.enter_context(nc.semaphore(name))

        ident = sb("ident", [P, P])
        lin_w = sb("lin_w", [P, LAYERS * D])
        edge_w2 = sb("edge_w2", [P, LAYERS * D])
        edge_w1 = sb("edge_w1", [DE + 1, LAYERS * D])
        out_w = sb("out_w", [P, D])
        ln_w = sb("ln_w", [P, LAYERS * D])
        ln_b = sb("ln_b", [P, LAYERS * D])
        last_bias = sb("last_bias", [P, D])
        carry = sb("carry", [3, LAYERS * D])
        zeros = sb("zeros", [P, 2000])
        dst_b = sb("dst_b", [P, TILES], i32)
        dst_b_prev = sb("dst_b_prev", [P, TILES], i32)
        dst_b_next = sb("dst_b_next", [P, TILES], i32)
        pos_b = sb("pos_b", [P, 3 * TILES])
        is_head_b = sb("is_head_b", [P, TILES])
        is_tail_b = sb("is_tail_b", [P, TILES])
        head_b = sb("head_b", [P, TILES])
        tail_b = sb("tail_b", [P, TILES])
        deg_b = sb("deg_b", [P, TILES])
        dis_b = sb("dis_b", [P, TILES])
        root_b = sb("root_b", [P, TILES])
        goes_on_b = sb("goes_on_b", [P, TILES])
        bias_row_b = sb("bias_row_b", [P, TILES])
        b2_row_b = sb("b2_row_b", [P, TILES])
        tmp_b = sb("tmp_b", [P, TILES])
        node_idx_b = sb("node_idx_b", [P, TILES], i32)
        node_row_b = sb("node_row_b", [P, 2 * TILES])
        seam = sb("seam", [P, 4])
        seam_row = sb("seam_row", [1, 4 * P])
        src_a = sb("src_a", [P, TILES], i32)
        dst_a = sb("dst_a", [P, TILES], i32)
        dst_a_prev = sb("dst_a_prev", [P, TILES], i32)
        dump_a = sb("dump_a", [P, TILES])
        ew_a = sb("ew_a", [P, TILES])
        is_head_a = is_tail_b
        tmp_a = tmp_b
        src_f = sb("src_f", [P, TILES])
        cols = sb("cols", [P, TILES * 4])
        cols_out = sb("cols_out", [P, TILES * 4])
        own = sb("own", [P, 2 * TILES])
        src_row_idx = sb("src_row_idx", [P, TILES], i32)
        x1_idx = sb("x1_idx", [P, TILES], i32)
        add_idx = sb("add_idx", [P, TILES], i32)
        earlier = sb("earlier", [P, TILES])
        before = sb("before", [P, GT * GE])
        dis_t = sb("dis_t", [TQ, GT * P])
        first_head = sb("first_head", [TQ, GT])
        first_idx = sb("first_idx", [TQ, GT], i32)
        first_v = sb("first_v", [TQ, GT * D])
        attr_s = sb("attr_s", [P, EP // 8])
        root_s = sb("root_s", [P, EP // 8])
        y, ho, x1, v_in, zz = (root_s[:, k * 2 * GE:(k + 1) * 2 * GE] for k in range(5))
        zT = root_s[:, 10 * GE:11 * GE]
        xin = sb("xin", [P, 2 * CW])
        xout = sb("xout", [P, 2 * CW])
        hT, rT, z2 = (xin[:, k * 2 * GE:(k + 1) * 2 * GE] for k in range(3))
        base = sb("base", [P, D])
        stage_idx = sb("stage_idx", [P, 2 * GT], i32)
        stage_idx2 = sb("stage_idx2", [P, 2 * GT], i32)
        stage_idx3 = sb("stage_idx3", [P, 2 * GT], i32)
        stage_row = sb("stage_row", [P, 2 * 2 * GT])
        stage_cols = sb("stage_cols", [P, 2 * 4 * GT])
        gat = sb("gat", [P, 2 * GE])
        rows = sb("rows", [P, 2 * GE], i32)
        rows_src = sb("rows_src", [P, 2 * GE], i32)
        attr = sb("attr", [DE + 1, 2 * GE])
        rank3 = sb("rank3", [3, 2 * GE])
        eq = sb("eq", [P, 2 * GE])
        same_src = attr_s
        z = sb("z", [P, GE])
        xd = sb("xd", [P, 2 * GE])
        ln_cols = sb("ln_cols", [P, 2 * LAYERS])
        stats = sb("stats", [P, GT * 6])
        rstats = sb("rstats", [P, GT * 6])
        rmv = sb("rmv", [P, 2 * GT * 2])
        rsc = sb("rsc", [P, 2 * GT * 2])
        mv = sb("mv", [P, 2 * GT * 2])
        sc = sb("sc", [P, 2 * GT * 2])
        eps = sb("eps", [P, 1])
        junk = root_s[:, 0:GT * GE]

        psT, psR, psZ = (ps(n) for n in ("psT", "psR", "psZ"))
        psH = ps("psH")
        psS = psZ
        psU = [[ps("psU00"), ps("psU01")], [ps("psU10"), ps("psU11")]]

        def sums(q, b, rows=P):
            return psU[q][b % 2][0:rows, (b // 2) * P:(b // 2 + 1) * P]

        def dram(name, shape, dt=f32):
            return nc.dram_tensor(name, shape, dt, kind="Internal").ap()

        node_tab = dram("node_tab", (N, 2))
        attr_d = dram("attr_d", (DE + 1, EP))
        rank3_d = dram("rank3_d", (3, EP))
        dis_d = dram("dis_d", (EP,))
        head_d = dram("head_d", (EP,))
        h_tab = [dram(f"h_tab{l}", (EP + 1, D)) for l in range(2)]
        v_tab = dram("v_tab", (EP + 1, D))
        out = t["out"]

        credits_ = sem("credits_")
        loaded = sem("loaded")
        zeroed = sem("zeroed")
        v_zeroed = sem("v_zeroed")
        dve_step = sem("dve_step")
        pool_step = sem("pool_step")
        seam_up = sem("seam_up")
        seam_flat = sem("seam_flat")
        seam_down = sem("seam_down")
        edge_ready = sem("edge_ready")
        edge_stored = sem("edge_stored")
        attr_loaded = sem("attr_loaded")
        attr_scaled = sem("attr_scaled")
        attr_stored = sem("attr_stored")
        turned_loaded = sem("turned_loaded")
        dis_turned = sem("dis_turned")
        tab_zeroed = [sem("tab_zeroed0"), sem("tab_zeroed1")]
        tab_free = [sem("tab_free0"), sem("tab_free1")]
        own_in = [sem("own_in0"), sem("own_in1")]
        own_kept = Count(sem("own_kept"))
        x_in = [sem("x_in0"), sem("x_in1")]
        x_based = Count(sem("x_based"))
        base_out = [sem("base_out0"), sem("base_out1")]
        dup_rows = [sem("dup_rows0"), sem("dup_rows1")]
        dup_done = Count(sem("dup_done"))
        idx_ready = sem("idx_ready")
        staged = sem("staged")
        gathered = [sem("gathered0"), sem("gathered1")]
        xd_in = [sem("xd_in0"), sem("xd_in1")]
        x1_out = [sem("x1_out0"), sem("x1_out1")]
        rows_in = [sem("rows_in0"), sem("rows_in1")]
        attr_in = [sem("attr_in0"), sem("attr_in1")]
        rank3_in = [sem("rank3_in0"), sem("rank3_in1")]
        stored = [sem("stored0"), sem("stored1")]
        var_ready = sem("var_ready")
        root_ready = sem("root_ready")
        sum_var = Count(sem("sum_var"))
        sum_root = Count(sem("sum_root"))
        row_var = Count(sem("row_var"))
        row_root = Count(sem("row_root"))
        normed = Count(sem("normed"))
        g_ready = Count(sem("g_ready"))
        T_done = Count(sem("T_done"))
        hT_ready = Count(sem("hT_ready"))
        R_done = Count(sem("R_done"))
        rT_ready = Count(sem("rT_ready"))
        Z_done = Count(sem("Z_done"))
        zr_ready = Count(sem("zr_ready"))
        z_ready = Count(sem("z_ready"))
        eq_ready = Count(sem("eq_ready"))
        U_done = Count(sem("U_done"), GT)
        carried = Count(sem("carried"), GT)
        stat_done = Count(sem("stat_done"), GT)
        U_free = Count(sem("U_free"))
        y_ready = Count(sem("y_ready"))
        act_done = Count(sem("act_done"))
        h_ready = Count(sem("h_ready"))
        x1_ready = Count(sem("x1_ready"))
        zz_ready = Count(sem("zz_ready"))
        T2_done = Count(sem("T2_done"))
        zT_ready = Count(sem("zT_ready"))
        V_done = Count(sem("V_done"))
        firsts_in = sem("firsts_in")
        firsts_out = sem("firsts_out")
        added = sem("added")
        v_loaded = [sem("v_loaded0"), sem("v_loaded1")]
        eqs_ready = Count(sem("eqs_ready"))
        M_done = Count(sem("M_done"))
        m_ready = Count(sem("m_ready"))
        C_done = Count(sem("C_done"))
        c_ready = Count(sem("c_ready"))

        def G(l, i, q):
            return i * 2 + (GROUPS * l + q)

        def cut(buf, q, b, w=P):
            return buf[:, (q * GT + b) * w:(q * GT + b + 1) * w]

        def part(buf, q, w=GE):
            return buf[:, q * w:(q + 1) * w]

        def shift(i, q, d):
            if isinstance(i, int) and not 0 <= i * 2 + q + d < GROUPS:
                return None
            return i + (q + d) // 2, (q + d) % 2

        def bodies(engine, body):
            for i in range(-2, 1):
                body(i, None)
            with engine.Fori(1, ITERS - 2) as i:
                body(i, 1)
            for i in range(ITERS - 2, ITERS + 1):
                body(i, None)

        block = ctx.enter_context(nc.Block())

        @block.sync
        def _(sp):
            def load(dst, src):
                sp.dma_start(dst, src).then_inc(loaded, 16)

            load(dst_b[:, :], t["dst_b"])
            load(dst_b_prev[:, :], t["dst_b_prev"])
            load(dst_b_next[:, :], t["dst_b_next"])
            for k in range(3):
                load(pos_b[:, k * TILES:(k + 1) * TILES], t["pos_b"][k])
            load(ident[:, :], t["ident"])
            load(src_a[:, :], t["src_a"])
            load(dst_a[:, :], t["dst_a"])
            load(dst_a_prev[:, :], t["dst_a_prev"])
            load(dump_a[:, :], t["dump_a"])
            load(ew_a[:, :], t["ew_a"])
            load(before[:, :], t["before"])
            load(lin_w[:, :].rearrange("p (l d) -> p l d", l=LAYERS), t["lin_w"].rearrange("l p d -> p l d"))
            load(edge_w2[:, :].rearrange("p (l d) -> p l d", l=LAYERS), t["edge_w2"].rearrange("l p d -> p l d"))
            load(edge_w1[:, :].rearrange("p (l d) -> p l d", l=LAYERS), t["edge_w1"].rearrange("l p d -> p l d"))
            load(out_w[:, :], t["out_w"])
            load(ln_w[:, :], t["ln_w"].rearrange("(o l) d -> o (l d)", o=1).broadcast_to([P, LAYERS * D]))
            load(ln_b[:, :], t["ln_b"].rearrange("(o l) d -> o (l d)", o=1).broadcast_to([P, LAYERS * D]))
            with nc.allow_non_contiguous_dma(reason="six columns"):
                load(ln_cols[:, 0:LAYERS], t["ln_w"].rearrange("l d -> d l"))
                load(ln_cols[:, LAYERS:2 * LAYERS], t["ln_b"].rearrange("l d -> d l"))
            load(last_bias[:, :], t["bias"][LAYERS - 1:LAYERS, :].broadcast_to([P, D]))
            load(carry[1:2, :], t["bias"].rearrange("(o l) d -> o (l d)", o=1))
            load(carry[2:3, :], t["edge_b2"].rearrange("(o l) d -> o (l d)", o=1))
            sp.dma_start(attr_s[:, :], t["attr_t"].rearrange("j (c r) -> (j c) r", c=8)).then_inc(attr_loaded, 16)

            sp.wait_ge(zeroed, 1)
            half = N // 2
            for q in range(2):
                sp.dma_start(node_tab[q * half:(q + 1) * half, :].rearrange("(p r) c -> p (r c)", p=50),
                             zeros[0:50, 0:2000]).then_inc(tab_zeroed[q], 16)
            for l in range(2):
                sp.dma_start(h_tab[l][0:1, :], zeros[0:1, 0:D]).then_inc(stored[l], 16)

            sp.dma_start(v_tab[0:1, :], zeros[0:1, 0:D]).then_inc(v_zeroed, 16)

            sp.wait_ge(edge_ready, 1)
            for dst, src in ((rank3_d[0], goes_on_b), (rank3_d[1], bias_row_b), (rank3_d[2], b2_row_b),
                             (attr_d[DE], root_b), (dis_d, dis_b), (head_d, head_b)):
                sp.dma_start(dst.rearrange("(p c) -> p c", c=TILES), src[:, :]).then_inc(edge_stored, 16)
            sp.wait_ge(edge_stored, 16 * 6)
            for j in range(DE):
                sp.dma_start(root_s[j * 8:(j + 1) * 8, :],
                             attr_d[DE].rearrange("(c r) -> c r", c=8)).then_inc(attr_loaded, 16)
            sp.dma_start(dis_t[:, :].rearrange("t (j p) -> t j p", j=GT),
                         dis_d.rearrange("(j t p) -> t j p", j=GT, p=P)).then_inc(turned_loaded, 16)
            with nc.allow_non_contiguous_dma(reason="one head row for each tile"):
                for j in range(GT):
                    sp.dma_start(first_head[:, j:j + 1],
                                 head_d.rearrange("(j t p) -> j t p", j=GT, p=P)[j, :, 0:1]).then_inc(turned_loaded, 16)

            xv = t["x"][0:P * RP, :].rearrange("(p r) d -> p (r d)", p=P)
            ov = out[0:P * RP, :].rearrange("(p r) d -> p (r d)", p=P)
            with sp.Fori(0, CHUNKS // 2) as i:
                for q in range(2):
                    sp.wait_ge(x_based.sem, x_based.free(i * 2 + q))
                    sp.dma_start(part(xin, q, CW), xv[:, bass.ds((i * 2 + q) * CW, CW)]).then_inc(x_in[q], 16)
                for q in range(2):
                    sp.wait_ge(x_based.sem, x_based.done(i * 2 + q))
                    sp.dma_start(ov[:, bass.ds((i * 2 + q) * CW, CW)], part(xout, q, CW)).then_inc(base_out[q], 16)
            sp.wait_ge(x_based.sem, x_based.free(CHUNKS))
            rest_in = xin[0:REST // 5, 0:5 * D]
            sp.dma_start(rest_in, t["x"][P * RP:N, :].rearrange("(p r) d -> p (r d)", r=5)).then_inc(x_in[0], 16)
            sp.wait_ge(x_based.sem, x_based.done(CHUNKS))
            sp.dma_start(out[P * RP:N, :].rearrange("(p r) d -> p (r d)", r=5),
                         xout[0:REST // 5, 0:5 * D]).then_inc(edge_stored, 16)
            sp.dma_start(out[DUMP:ROWS_OUT, :].rearrange("(p r) d -> p (r d)", p=P),
                         zeros[:, 0:GT * D]).then_inc(edge_stored, 16)
            sp.dma_start(out[N:N + 1, :], zeros[0:1, 0:D]).then_inc(edge_stored, 16)

            with sp.Fori(0, ITERS) as i:
                for q in range(2):
                    sp.wait_ge(dup_done.sem, dup_done.free(i * 2 + q))
                    sp.dma_start(part(rows_src, q), t["src_row"][0:1, bass.ds((i * 2 + q) * GE, GE)]
                                 .broadcast_to([P, GE])).then_inc(dup_rows[q], 16)
            sp.wait_ge(attr_scaled, 1)
            sp.dma_start(attr_d[0:DE].rearrange("j (c r) -> (j c) r", c=8), attr_s[:, :]).then_inc(attr_stored, 16)
            sp.wait_ge(attr_stored, 16)

            def load_attr(l, i, q):
                sp.wait_ge(R_done.sem, R_done.free(G(l, i, q)))
                sp.dma_start(part(attr, q), attr_d[:, bass.ds(i * (-2 * GE) + (GROUPS - 1 - q) * GE, GE)]
                             ).then_inc(attr_in[q], 16)

            def load_rows(l, i, q):
                at = i * (-2 * GE) + (GROUPS - 1 - q) * GE
                n = G(l, i, q)
                sp.wait_ge(eq_ready.sem, eq_ready.free(n))
                sp.dma_start(part(rows, q), t["dst_row"][0:1, bass.ds(at, GE)]
                             .broadcast_to([P, GE])).then_inc(rows_in[q], 16)
                sp.wait_ge(U_done.sem, U_done.free(n))
                sp.dma_start(part(rank3, q), rank3_d[:, bass.ds(at, GE)]).then_inc(rank3_in[q], 16)

            for l in range(LAYERS):
                load_attr(l, 0, 0)
                with sp.Fori(0, ITERS - 1) as i:
                    load_attr(l, i, 1)
                    load_rows(l, i, 0)
                    load_attr(l, i + 1, 0)
                    load_rows(l, i, 1)
                load_attr(l, ITERS - 1, 1)
                load_rows(l, ITERS - 1, 0)
                load_rows(l, ITERS - 1, 1)

            sp.wait_ge(firsts_in, 16 * GT)
            for j in range(GT):
                sp.dma_start(v_tab[1:EP + 1, :].rearrange("(j t p) d -> j t p d", j=GT, p=P)[j, :, 0, :],
                             first_v[:, j * D:(j + 1) * D]).then_inc(firsts_out, 16)
            sp.wait_ge(firsts_out, 16 * GT)
            with sp.Fori(0, ITERS) as i:
                for q in range(2):
                    n = i * 2 + q
                    at = n * GE
                    sp.wait_ge(eqs_ready.sem, eqs_ready.free(n))
                    sp.wait_ge(M_done.sem, M_done.free(n))
                    sp.dma_start(part(rows, q), t["dst_row"][0:1, bass.ds(at, GE)]
                                 .broadcast_to([P, GE])).then_inc(v_loaded[q], 16)
                    sp.dma_start(part(rows_src, q), t["src_row"][0:1, bass.ds(at, GE)]
                                 .broadcast_to([P, GE])).then_inc(v_loaded[q], 16)
                    sp.dma_start(part(v_in, q).rearrange("p (b d) -> p b d", b=GT),
                                 v_tab[1:EP + 1, :].rearrange("(n p) d -> p n d", p=P)[:, bass.ds(n * GT, GT), :]
                                 ).then_inc(v_loaded[q], 16)

        @block.gpsimd
        def _(pool):
            steps = [0]

            def hold(s, value):
                if isinstance(value, int):
                    pool.wait_ge(s, value)
                    return
                r = pool.to_reg(value)
                pool.wait_ge(credits_, 1)
                pool.wait_ge(s, r)

            def peeled(body):
                body(0, True)
                with pool.Fori(1, ITERS) as i:
                    body(i, False)

            pool.memset(zeros[:, :], 0.0).then_inc(zeroed, 1)
            pool.memset(gat[:, :], 0.0)
            pool.memset(xd[:, :], 0.0)
            pool.memset(stage_row[:, :], 0.0)
            pool.memset(own[:, :], 0.0)
            pool.memset(carry[0:1, :], 0.0).then_inc(pool_step, 1)
            node_bound = pool.to_reg(N - 1)
            tab_bound = pool.to_reg(EP)
            out_bound = pool.to_reg(ROWS_OUT - 1)
            pool.wait_ge(pool_step, 1)

            pool.wait_ge(edge_ready, 1)
            for q in range(2):
                pool.wait_ge(tab_zeroed[q], 16)

            def fill_node_tab(i, first):
                for q in range(2):
                    if not first:
                        hold(tab_free[q], i * (16 * GT))
                    pool.tensor_copy(part(stage_idx, q, GT), node_idx_b[:, bass.ds((i * 2 + q) * GT, GT)])
                    pool.tensor_copy(part(stage_row, q, 2 * GT),
                                     node_row_b[:, bass.ds((i * 2 + q) * (2 * GT), 2 * GT)]).then_inc(staged, 1)
                    hold(staged, i * 2 + (q + 1))
                    for b in range(GT):
                        pool.indirect_dma_start(
                            node_tab[:, :], bass.IndirectOffsetOnAxis(ap=cut(stage_idx, q, b, 1), axis=0),
                            cut(stage_row, q, b, 2), None, bounds_check=node_bound,
                            oob_is_err=False).then_inc(tab_free[q], 16)

            peeled(fill_node_tab)
            for q in range(2):
                pool.wait_ge(tab_free[q], 16 * GT * ITERS)

            with pool.Fori(0, ITERS) as i:
                for q in range(2):
                    hold(own_kept.sem, own_kept.free(i * 2 + q))
                    pool.tensor_copy(part(stage_idx, q, GT),
                                     src_a[:, bass.ds((i * 2 + q) * GT, GT)]).then_inc(staged, 1)
                    hold(staged, i * 2 + (2 * ITERS + q + 1))
                    for b in range(GT):
                        pool.indirect_dma_start(
                            cut(stage_row, q, b, 2), None, node_tab[:, :],
                            bass.IndirectOffsetOnAxis(ap=cut(stage_idx, q, b, 1), axis=0),
                            bounds_check=node_bound, oob_is_err=False).then_inc(own_in[q], 16)
            pool.wait_ge(own_kept.sem, own_kept.done(GROUPS - 1))
            pool.wait_ge(idx_ready, 1)
            steps[0] = 4 * ITERS

            for l in range(LAYERS):
                last = l == LAYERS - 1
                if l:
                    for q in range(2):
                        pool.wait_ge(stored[q], 16 + 16 * ITERS * l)
                if last:
                    for q in range(2):
                        pool.wait_ge(base_out[q], 16 * (CHUNKS // 2))
                    pool.wait_ge(edge_stored, 16 * 9)
                idx = src_a if l == 0 else src_row_idx
                table, bound = (t["x"], node_bound) if l == 0 else (h_tab[l - 1], tab_bound)

                def fetch(i, q, value):
                    at = i * (-2 * GT) + (GROUPS - 1 - q) * GT
                    hold(T_done.sem, T_done.free(G(l, i, q)))
                    pool.tensor_copy(part(stage_idx, q, GT), idx[:, bass.ds(at, GT)]).then_inc(staged, 1)
                    hold(staged, value)
                    for b in reversed(range(GT)):
                        pool.indirect_dma_start(
                            cut(gat, q, b), None, table[:, :],
                            bass.IndirectOffsetOnAxis(ap=cut(stage_idx, q, b, 1), axis=0),
                            bounds_check=bound, oob_is_err=False).then_inc(gathered[q], 16)

                def stage_sent(i, q):
                    return pool.tensor_copy(part(stage_idx3, q, GT),
                                            x1_idx[:, bass.ds(i * (-2 * GT) + (GROUPS - 1 - q) * GT, GT)])

                def fetch_x(i, q, value):
                    at = i * (-2 * GT) + (GROUPS - 1 - q) * GT
                    if shift(i, q, -2):
                        hold(x1_out[q], i * (16 * GT))
                    sent = shift(i, q, -1)
                    if sent:
                        stage_sent(*sent)
                    pool.tensor_copy(part(stage_idx2, q, GT), dst_a[:, bass.ds(at, GT)]).then_inc(staged, 1)
                    hold(staged, value)
                    for b in range(GT):
                        pool.indirect_dma_start(
                            cut(xd, q, b), None, t["x"][:, :],
                            bass.IndirectOffsetOnAxis(ap=cut(stage_idx2, q, b, 1), axis=0),
                            bounds_check=node_bound, oob_is_err=False).then_inc(xd_in[q], 16)
                    if sent:
                        send_x1(*sent)

                def send_x1(i, q):
                    hold(x1_ready.sem, x1_ready.done(i * 2 + q))
                    for b in range(GT):
                        pool.indirect_dma_start(
                            out[:, :], bass.IndirectOffsetOnAxis(ap=cut(stage_idx3, q, b, 1), axis=0),
                            cut(x1, q, b), None, bounds_check=node_bound,
                            oob_is_err=False).then_inc(x1_out[q], 16)

                if not last:
                    with pool.Fori(0, ITERS) as i:
                        for q in range(2):
                            fetch(i, q, i * 2 + (steps[0] + q + 1))
                    steps[0] += 2 * ITERS
                    continue
                def body(i, value):
                    for q in range(2):
                        fetch(i, q, value + (2 * q + 1))
                        fetch_x(i - 2, q, value + (2 * q + 2))

                for n in range(4):
                    fetch(n // 2, n % 2, steps[0] + n + 1)
                body(2, steps[0] + 4)
                with pool.Fori(3, ITERS) as i:
                    body(i, i * 4 + (steps[0] - 4))
                steps[0] += 4 * ITERS - 4
                for n in range(4):
                    fetch_x(ITERS - 2 + n // 2, n % 2, steps[0] + n + 1)
                steps[0] += 5
                stage_sent(ITERS - 1, 1).then_inc(staged, 1)
                hold(staged, steps[0])
                send_x1(ITERS - 1, 1)

            for q in range(2):
                pool.wait_ge(stored[q], 16 + 16 * ITERS * LAYERS)
                pool.wait_ge(x1_out[q], 16 * GT * ITERS)
            pool.wait_ge(v_zeroed, 16)
            for j in range(GT):
                pool.indirect_dma_start(
                    first_v[:, j * D:(j + 1) * D], None, v_tab[:, :],
                    bass.IndirectOffsetOnAxis(ap=first_idx[:, j:j + 1], axis=0),
                    bounds_check=tab_bound, oob_is_err=False).then_inc(firsts_in, 16)

            assert steps[0] == STAGED_BEFORE, steps[0]
            def add_messages(i, first):
                for q in range(2):
                    n = i * 2 + q
                    hold(c_ready.sem, c_ready.done(n))
                    if q or not first:
                        hold(added, n * (16 * GT))
                    pool.tensor_copy(part(stage_idx, 0, GT), add_idx[:, bass.ds(n * GT, GT)]).then_inc(staged, 1)
                    hold(staged, n + (steps[0] + 1))
                    for b in range(GT):
                        pool.indirect_dma_start(
                            out[:, :], bass.IndirectOffsetOnAxis(ap=cut(stage_idx, 0, b, 1), axis=0),
                            cut(ho, q, b), None, bounds_check=out_bound,
                            oob_is_err=True, compute_op=ALU.add).then_inc(added, 16)

            peeled(add_messages)
            pool.wait_ge(added, 16 * GT * GROUPS)

        @block.vector
        def _(dve):
            v = nc.vector
            chain = [0]

            def link(ins):
                chain[0] += 1
                ins.then_inc(dve_step, 1)
                dve.wait_ge(dve_step, chain[0])

            for c in (sum_var, sum_root, row_var, row_root, own_kept, x_based, dup_done, normed, g_ready, T_done, hT_ready, R_done, rT_ready,
                      Z_done, zr_ready, z_ready, eq_ready, U_done, carried, stat_done, U_free, y_ready, act_done, h_ready,
                      x1_ready, zz_ready, T2_done, zT_ready, V_done, eqs_ready, M_done, m_ready, C_done,
                      c_ready):
                dve.sem_inc(c.sem, c.credit)
            dve.sem_inc(credits_, 1)
            v.memset(eps[:, :], LN_EPS)

            dve.wait_ge(loaded, 16 * 24)
            pos1, tile0, tile1 = (pos_b[:, k * TILES:(k + 1) * TILES] for k in range(3))
            v.tensor_tensor(is_head_b[:, :], dst_b[:, :], dst_b_prev[:, :], ALU.not_equal)
            link(v.tensor_tensor(is_tail_b[:, :], dst_b[:, :], dst_b_next[:, :], ALU.not_equal))
            v.tensor_tensor(tmp_b[:, :], is_head_b[:, :], pos1, ALU.mult)
            link(v.scalar_tensor_tensor(tail_b[:, :], pos1, -FAR, is_tail_b[:, :], ALU.add, ALU.mult))
            link(v.tensor_scalar(tail_b[:, :], tail_b[:, :], FAR, None, ALU.add))
            v.tensor_tensor_scan(head_b[:, :], tmp_b[:, :], tmp_b[:, :], 0.0, ALU.max, ALU.max)
            link(v.tensor_tensor_scan(tail_b[:, ::-1], tail_b[:, ::-1], tail_b[:, ::-1], FAR, ALU.min, ALU.min))
            v.tensor_copy(seam[:, 0:1], head_b[:, TILES - 1:TILES])
            v.tensor_copy(seam[:, 1:2], tail_b[:, 0:1]).then_inc(seam_up, 1)
            dve.wait_ge(seam_flat, 1)
            v.tensor_copy(seam_row[0:1, 0:P], psS[0:1, 0:P])
            link(v.tensor_copy(seam_row[0:1, P:2 * P], psS[0:1, P:2 * P]))
            v.memset(seam_row[0:1, 2 * P:2 * P + 1], 0.0)
            v.memset(seam_row[0:1, 4 * P - 1:4 * P], FAR)
            v.tensor_tensor_scan(seam_row[0:1, 2 * P + 1:3 * P], seam_row[0:1, 0:P - 1], seam_row[0:1, 0:P - 1],
                                 0.0, ALU.max, ALU.max)
            v.tensor_tensor_scan(seam_row[0:1, 3 * P:4 * P - 1][:, ::-1], seam_row[0:1, P + 1:2 * P][:, ::-1],
                                 seam_row[0:1, P + 1:2 * P][:, ::-1], FAR, ALU.min, ALU.min).then_inc(seam_up, 1)
            dve.wait_ge(seam_down, 1)
            link(v.tensor_copy(seam[:, 2:4], psS[:, 2 * P:2 * P + 2]))
            v.tensor_scalar(head_b[:, :], head_b[:, :], seam[:, 2:3], None, ALU.max)
            link(v.tensor_scalar(tail_b[:, :], tail_b[:, :], seam[:, 3:4], None, ALU.min))
            link(v.scalar_tensor_tensor(deg_b[:, :], tail_b[:, :], 1.0, head_b[:, :], ALU.add, ALU.subtract))
            v.engine_nop().then_inc(var_ready, 1)
            dve.wait_ge(root_ready, 1)
            link(v.reciprocal(dis_b[:, :], root_b[:, :]))
            v.tensor_tensor(goes_on_b[:, :], tail_b[:, :], tile1, ALU.is_gt)
            v.tensor_tensor(tmp_b[:, :], head_b[:, :], tile0, ALU.max)
            link(v.tensor_tensor(b2_row_b[:, :], tail_b[:, :], tile1, ALU.min))
            link(v.scalar_tensor_tensor(b2_row_b[:, :], b2_row_b[:, :], 1.0, tmp_b[:, :], ALU.add, ALU.subtract))
            v.tensor_tensor(b2_row_b[:, :], b2_row_b[:, :], root_b[:, :], ALU.mult)
            link(v.tensor_scalar(bias_row_b[:, :], goes_on_b[:, :], -1.0, 1.0, ALU.mult, ALU.add))
            v.tensor_tensor(bias_row_b[:, :], bias_row_b[:, :], root_b[:, :], ALU.mult)
            row2 = node_row_b[:, :].rearrange("p (c k) -> p c k", k=2)
            v.tensor_copy(row2[:, :, 0], pos1)
            v.tensor_copy(row2[:, :, 1], deg_b[:, :])
            link(v.scalar_tensor_tensor(tmp_b[:, :], dst_b[:, :], -float(SKIP), is_head_b[:, :], ALU.add, ALU.mult))
            v.tensor_scalar(node_idx_b[:, :], tmp_b[:, :], float(SKIP), None, ALU.add).then_inc(edge_ready, 1)

            cc = cols[:, :].rearrange("p (c k) -> p c k", k=4)
            co = cols_out[:, :].rearrange("p (c k) -> p c k", k=4)
            v.tensor_copy(cc[:, :, 0], dst_a[:, :])
            v.tensor_copy(co[:, :, 0], dst_a[:, :])
            v.tensor_copy(co[:, :, 2], src_a[:, :])
            v.tensor_copy(src_f[:, :], src_a[:, :])
            v.tensor_copy(co[:, :, 3], ew_a[:, :])
            link(v.tensor_tensor(is_head_a[:, :], dst_a[:, :], dst_a_prev[:, :], ALU.not_equal))
            link(v.tensor_copy(co[:, :, 1], is_head_a[:, :]))
            v.memset(co[0:1, :, 1], 1.0)
            link(v.scalar_tensor_tensor(tmp_a[:, :], dst_a[:, :], -float(SKIP), is_head_a[:, :], ALU.add, ALU.mult))
            link(v.tensor_scalar(x1_idx[:, :], tmp_a[:, :], float(SKIP), None, ALU.add))
            dve.wait_ge(turned_loaded, 16 * (GT + 1))
            v.tensor_copy(first_idx[:, :], first_head[:, :])
            dve.wait_ge(dis_turned, 1)
            link(v.tensor_copy(cc[:, :, 1], psR[:, 0:TILES]))
            v.tensor_tensor(cc[:, :, 2], cc[:, :, 1], cc[:, :, 1], ALU.mult)
            dve.wait_ge(attr_loaded, 16 * (DE + 1))
            v.tensor_tensor(attr_s[:, :], attr_s[:, :], root_s[:, :], ALU.mult).then_inc(attr_scaled, 1)

            L2 = slice((LAYERS - 1) * D, LAYERS * D)
            link(v.bn_stats(stats[:, 0:6], last_bias[:, :]))
            link(v.bn_aggr(mv[:, 0:2], stats[:, 0:6]))
            v.engine_nop().then_inc(var_ready, 1)
            dve.wait_ge(root_ready, 2)
            link(v.reciprocal(sc[:, 0:1], sc[:, 2:3]))
            link(v.scalar_tensor_tensor(base[:, :], last_bias[:, :], mv[:, 0:1], ln_w[:, L2], ALU.subtract, ALU.mult))
            link(v.scalar_tensor_tensor(base[:, :], base[:, :], sc[:, 0:1], ln_b[:, L2], ALU.mult, ALU.add))
            link(v.tensor_scalar(base[:, :], base[:, :], 0.0, None, ALU.max))

            def add_base(q, parts, n):
                xi = xin[0:parts, q * CW:q * CW + n * D].rearrange("p (r d) -> p r d", d=D)
                xo = xout[0:parts, q * CW:q * CW + n * D].rearrange("p (r d) -> p r d", d=D)
                bb = base[0:parts, :].rearrange("p (o d) -> p o d", o=1).broadcast_to([parts, n, D])
                return v.tensor_tensor(xo, xi, bb, ALU.add)

            for q in range(2):
                dve.wait_ge(x_in[q], 16)
                add_base(q, P, CR).then_inc(x_based.sem, 1)
            with dve.Fori(1, CHUNKS // 2) as i:
                for q in range(2):
                    dve.wait_ge(x_in[q], i * 16 + 16)
                    dve.wait_ge(base_out[q], i * 16)
                    add_base(q, P, CR).then_inc(x_based.sem, 1)
            dve.wait_ge(x_in[0], 16 * (CHUNKS // 2 + 1))
            dve.wait_ge(base_out[0], 16 * (CHUNKS // 2))
            add_base(0, REST // 5, 5).then_inc(x_based.sem, 1)

            with dve.Fori(0, ITERS) as i:
                for q in range(2):
                    n = i * 2 + q
                    dve.wait_ge(dup_rows[q], i * 16 + 16)
                    dve.wait_ge(dup_done.sem, dup_done.done(n) - 1)
                    for b in range(GT):
                        ins = v.scalar_tensor_tensor(
                            junk[:, b * GE:(b + 1) * GE], part(rows_src, q), src_f[:, bass.ds(n * GT + b, 1)],
                            before[:, b * GE:(b + 1) * GE], ALU.is_equal, ALU.mult,
                            accum_out=earlier[:, bass.ds(n * GT + b, 1)])
                    ins.then_inc(dup_done.sem, 1)
            dve.wait_ge(dup_done.sem, dup_done.done(GROUPS - 1))
            v.tensor_tensor(tmp_a[:, :], src_f[:, :], dump_a[:, :], ALU.subtract)
            link(v.tensor_scalar(earlier[:, :], earlier[:, :], 0.0, None, ALU.is_equal))
            link(v.tensor_tensor(tmp_a[:, :], tmp_a[:, :], earlier[:, :], ALU.mult))
            link(v.tensor_tensor(add_idx[:, :], tmp_a[:, :], dump_a[:, :], ALU.add))
            dve.wait_ge(own_kept.sem, own_kept.done(GROUPS - 1))
            ow = own[:, :].rearrange("p (c k) -> p c k", k=2)
            v.tensor_copy(src_row_idx[:, :], ow[:, :, 0])
            v.tensor_scalar(earlier[:, :], ow[:, :, 1], 0.0, None, ALU.is_gt)
            v.tensor_scalar(tmp_a[:, :], ow[:, :, 1], 1e-30, None, ALU.max).then_inc(var_ready, 1)
            dve.wait_ge(root_ready, 3)
            link(v.reciprocal(tmp_a[:, :], tmp_a[:, :]))
            link(v.tensor_tensor(cc[:, :, 3], tmp_a[:, :], earlier[:, :], ALU.mult))
            v.engine_nop().then_inc(idx_ready, 1)

            for l in range(LAYERS):
                first, last = l == 0, l == LAYERS - 1
                LW = slice(l * D, (l + 1) * D)
                K = (14, 8, 16)[l]
                turn = [None, 0, 0]

                def mark(ins):
                    if turn[0] is None:
                        chain[0] += 1
                        value = chain[0]
                    else:
                        turn[2] += 1
                        value = turn[0] * K + (chain[0] - turn[1] * K + turn[2])
                    ins.then_inc(dve_step, 1)
                    return value

                def after(value, alone=False):
                    settle(dve_step, value, alone)

                def step(ins, alone=False):
                    after(mark(ins), alone)

                def settle(s, value, alone=True):
                    if alone and not isinstance(value, int):
                        value = dve.to_reg(value)
                        dve.wait_ge(credits_, 1)
                    dve.wait_ge(s, value)

                def mvs(q):
                    return part(mv, q, 2 * GT).rearrange("p (b k) -> p b k", k=2)

                def scs(q):
                    return part(sc, q, 2 * GT).rearrange("p (b k) -> p b k", k=2)

                def scalars(i, q, c):
                    return cols[:, bass.ds(i * (-8 * GT) + (GROUPS - 1 - q) * (4 * GT), 4 * GT)].rearrange(
                        "p (b k) -> p b k", k=4)[:, :, c]

                def col(buf, q, b, c, w):
                    at = (q * GT + b) * w + c
                    return buf[:, at:at + 1]

                def row_stats(buf, q):
                    for b in range(GT):
                        ins = v.bn_stats(rstats[:, 6 * b:6 * b + 6], cut(buf, q, b))
                    return mark(ins)

                def row_vars(q, value):
                    after(value, alone=True)
                    r = part(rmv, q, 2 * GT).rearrange("p (b k) -> p b k", k=2)
                    for b in range(GT):
                        ins = v.bn_aggr(r[:, b, :], rstats[:, 6 * b:6 * b + 6])
                    ins.then_inc(row_var.sem, 1)

                def row_scales(q, at, done, extra):
                    r = part(rmv, q, 2 * GT).rearrange("p (b k) -> p b k", k=2)
                    s2 = part(rsc, q, 2 * GT).rearrange("p (b k) -> p b k", k=2)
                    dve.wait_ge(row_root.sem, row_root.done(at))
                    step(v.reciprocal(s2[:, :, 0], s2[:, :, 0]))
                    if extra is not None:
                        step(v.tensor_tensor(s2[:, :, 0], s2[:, :, 0], extra, ALU.mult))
                    v.scalar_tensor_tensor(s2[:, :, 1], r[:, :, 0], -1.0, s2[:, :, 0],
                                           ALU.mult, ALU.mult).then_inc(done.sem, 1)

                def norm_stats(i, q):
                    dve.wait_ge(g_ready.sem, g_ready.free(G(l, i, q)))
                    dve.wait_ge(gathered[q], i * (16 * GT) + 16 * GT)
                    return row_stats(gat, q)

                def columns(i, q):
                    return mark(v.tensor_copy(part(stage_cols, q, 4 * GT),
                                              cols[:, bass.ds(i * (-8 * GT) + (GROUPS - 1 - q) * (4 * GT), 4 * GT)]))

                def equal(i, q, bs):
                    n = G(l, i, q)
                    if bs[0] == GT - 1:
                        dve.wait_ge(rows_in[q], i * 16 + (16 * (ITERS * l + 1)))
                        dve.wait_ge(U_done.sem, U_done.free(n))
                    for b in bs:
                        ins = v.tensor_scalar(cut(eq, q, b), cut(rows, q, b), col(stage_cols, q, b, 0, 4),
                                              None, ALU.is_equal)
                    if bs[-1] == 0:
                        ins.then_inc(eq_ready.sem, 1)

                def join(i, q):
                    n = G(l, i, q)
                    dve.wait_ge(zr_ready.sem, zr_ready.done(G(l - 1, i, q)))
                    for b in reversed(range(GT)):
                        zb = z[:, b * P:(b + 1) * P]
                        ins = v.scalar_tensor_tensor(cut(z2, q, b), psH[:, b * P:(b + 1) * P],
                                                     col(stage_cols, q, b, 3, 4), zb, ALU.mult, ALU.add)
                    ins.then_inc(z_ready.sem, 1)

                def take(i, q, s):
                    b = GT - 1 - s
                    dve.wait_ge(U_done.sem, U_done.done(G(l, i, q), s + 1))
                    v.tensor_copy(carry[0:1, LW], sums(q, b, 1)).then_inc(carried.sem, 1)
                    v.bn_stats(stats[:, 6 * b:6 * b + 6], sums(q, b)).then_inc(stat_done.sem, 1)

                def sum_vars(i, q):
                    n = G(l, i, q)
                    settle(stat_done.sem, stat_done.done(n))
                    for b in range(GT):
                        ins = v.bn_aggr(mvs(q)[:, b, :], stats[:, 6 * b:6 * b + 6])
                    step(ins)
                    dve.wait_ge(act_done.sem, act_done.free(n))
                    v.tensor_tensor(scs(q)[:, :, 0], mvs(q)[:, :, 1], scalars(i, q, 2), ALU.mult
                                    ).then_inc(sum_var.sem, 1)

                def scale1(i, q):
                    dve.wait_ge(sum_root.sem, sum_root.done(G(l, i, q)))
                    return mark(v.reciprocal(scs(q)[:, :, 0], scs(q)[:, :, 0]))

                def scale2(i, q):
                    return mark(v.tensor_tensor(scs(q)[:, :, 0], scs(q)[:, :, 0], scalars(i, q, 1), ALU.mult))

                def scale3(i, q):
                    v.scalar_tensor_tensor(scs(q)[:, :, 1], mvs(q)[:, :, 0], -1.0, scs(q)[:, :, 0],
                                           ALU.mult, ALU.mult).then_inc(y_ready.sem, 1)

                def centred(i, q):
                    for b in range(GT):
                        ins = v.scalar_tensor_tensor(cut(y, q, b), sums(q, b), col(mv, q, b, 0, 2),
                                                     ln_w[:, LW], ALU.subtract, ALU.mult)
                    ins.then_inc(U_free.sem, 1)

                def affine(i, q):
                    dve.wait_ge(U_free.sem, U_free.done(i * 2 + q))
                    for b in range(GT):
                        ins = v.scalar_tensor_tensor(cut(y, q, b), cut(y, q, b), col(sc, q, b, 0, 2),
                                                     ln_b[:, LW], ALU.mult, ALU.add)
                    return mark(ins)

                def make_x1(i, q):
                    dve.wait_ge(xd_in[q], i * (16 * GT) + 16 * GT)
                    dve.wait_ge(zz_ready.sem, zz_ready.free(i * 2 + q))
                    return mark(v.scalar_tensor_tensor(part(x1, q), part(y, q), 0.0, part(xd, q), ALU.max, ALU.add))

                def one(i, q):
                    this, before, nx, rows3 = (shift(i, q, d) for d in (0, -1, 1, 3))
                    rows3 = rows3 if first else None
                    if nx:
                        value = columns(*nx)
                    if before:
                        value = scale1(*before)
                    if this:
                        take(*this, 0)
                    if before or nx:
                        after(value)
                    if before:
                        value = scale2(*before)
                    if nx:
                        equal(*nx, (3, 2))
                    if before:
                        after(value)
                        if last:
                            centred(*before)
                        else:
                            scale3(*before)
                    if this:
                        take(*this, 1)
                    if nx:
                        equal(*nx, (1, 0))
                    if last and before:
                        y_value = affine(*before)
                    if this:
                        take(*this, 2)
                    if rows3:
                        r_value = norm_stats(*rows3)
                    if nx and not first:
                        join(*nx)
                    if last and before:
                        after(y_value)
                        x_value = make_x1(*before)
                    if this:
                        take(*this, 3)
                    if last and before:
                        after(x_value, alone=True)
                        r_value = row_stats(x1, before[1])
                    if this:
                        sum_vars(*this)
                    if rows3:
                        row_vars(rows3[1], r_value)
                        row_scales(rows3[1], G(l, *rows3), normed, scalars(*rows3, 3))
                    if last and before:
                        row_vars(before[1], r_value)
                        row_scales(before[1], before[0] * 2 + (GROUPS + before[1]), x1_ready, None)

                def body(i, lo):
                    turn[:] = [i, lo, 0] if lo is not None else [None, 0, 0]
                    for q in range(2):
                        one(i, q)
                    if lo is not None:
                        assert turn[2] == K, (l, turn[2])
                        chain[0] += K * (ITERS - 3)

                bodies(dve, body)

            start = chain[0]
            with dve.Fori(0, ITERS) as i:
                for q in range(2):
                    n = i * 2 + q
                    dve.wait_ge(m_ready.sem, m_ready.free(n))
                    v.tensor_copy(part(stage_cols, q, 4 * GT),
                                  cols_out[:, bass.ds(n * (4 * GT), 4 * GT)]).then_inc(dve_step, 1)
                    dve.wait_ge(dve_step, n + (start + 1))
                    dve.wait_ge(v_loaded[q], i * 48 + 48)
                    dve.wait_ge(C_done.sem, C_done.free(n))
                    for b in range(GT):
                        c0 = (q * GT + b) * 4
                        v.tensor_scalar(cut(eq, q, b), cut(rows, q, b), stage_cols[:, c0:c0 + 1],
                                        stage_cols[:, c0 + 1:c0 + 2], ALU.is_equal, ALU.mult)
                        ins = v.tensor_scalar(cut(same_src, q, b, GE), part(rows_src, q),
                                              stage_cols[:, c0 + 2:c0 + 3], None, ALU.is_equal)
                    ins.then_inc(eqs_ready.sem, 1)

        @block.scalar
        def _(act):
            a = nc.scalar
            act.wait_ge(credits_, 1)
            act.wait_ge(pool_step, 1)
            act.wait_ge(var_ready, 1)
            a.activation(root_b[:, :], deg_b[:, :], ACT.Sqrt).then_inc(root_ready, 1)
            act.wait_ge(var_ready, 2)
            a.activation(sc[:, 2:3], mv[:, 1:2], ACT.Sqrt, bias=eps[:, :]).then_inc(root_ready, 1)
            with act.Fori(0, ITERS) as i:
                for q in range(2):
                    act.wait_ge(own_in[q], i * (16 * GT) + 16 * GT)
                    a.copy(own[:, bass.ds((i * 2 + q) * (2 * GT), 2 * GT)],
                           part(stage_row, q, 2 * GT)).then_inc(own_kept.sem, 1)

            act.wait_ge(var_ready, 3)
            a.activation(tmp_a[:, :], tmp_a[:, :], ACT.Sqrt).then_inc(root_ready, 1)

            def roots(done, to, var, q):
                s = part(to, q, 2 * GT).rearrange("p (b k) -> p b k", k=2)[:, :, 0]
                a.activation(s, var, ACT.Sqrt, bias=eps[:, :]).then_inc(done.sem, 1)

            def second(buf, q, c):
                return part(buf, q, 2 * GT).rearrange("p (b k) -> p b k", k=2)[:, :, c]

            for l in range(LAYERS):
                first, last = l == 0, l == LAYERS - 1
                table = v_tab if last else h_tab[l]

                def norm_root(i, q):
                    act.wait_ge(row_var.sem, row_var.done(G(l, i, q)))
                    roots(row_root, rsc, second(rmv, q, 1), q)

                def norm(i, q):
                    act.wait_ge(normed.sem, normed.done(G(l, i, q)))
                    for b in range(GT):
                        c = (q * GT + b) * 2
                        ins = a.activation(cut(gat, q, b), cut(gat, q, b), ACT.Relu,
                                           bias=rsc[:, c + 1:c + 2], scale=rsc[:, c:c + 1])
                    ins.then_inc(g_ready.sem, 1)

                def turned(i, q):
                    act.wait_ge(T_done.sem, T_done.done(G(l, i, q)))
                    if first:
                        a.copy(part(hT, q), psT[:, :]).then_inc(hT_ready.sem, 1)
                    else:
                        a.activation(part(hT, q), psT[:, :], ACT.Relu, bias=ln_cols[:, LAYERS + l - 1:LAYERS + l],
                                     scale=ln_cols[:, l - 1:l]).then_inc(hT_ready.sem, 1)

                def mlp(i, q):
                    act.wait_ge(R_done.sem, R_done.done(G(l, i, q)))
                    a.activation(part(rT, q), psR[:, :], ACT.Relu).then_inc(rT_ready.sem, 1)

                def keep_z(i, q):
                    n = G(l, i, q)
                    act.wait_ge(Z_done.sem, Z_done.done(n))
                    if first:
                        act.wait_ge(U_done.sem, U_done.free(n))
                        a.copy(part(z2, q), psZ[:, :]).then_inc(z_ready.sem, 1)
                    else:
                        act.wait_ge(z_ready.sem, z_ready.done(n) - 1)
                        a.copy(z[:, :], psZ[:, :]).then_inc(zr_ready.sem, 1)

                def store(i, q):
                    act.wait_ge(act_done.sem, act_done.done(G(l, i, q)))
                    act.dma_start(
                        table[1:EP + 1, :].rearrange("(c p) d -> p c d", p=P)[
                            :, bass.ds(i * (-2 * GT) + (GROUPS - 1 - q) * GT, GT), :],
                        part(ho, q).rearrange("p (b d) -> p b d", b=GT)).then_inc(stored[q], 16)

                def sum_roots(i, q):
                    act.wait_ge(sum_var.sem, sum_var.done(G(l, i, q)))
                    roots(sum_root, sc, second(sc, q, 0), q)

                def keep_normed(i, q):
                    act.wait_ge(y_ready.sem, y_ready.done(G(l, i, q)))
                    act.wait_ge(stored[q], i * 16 + (16 + 16 * ITERS * l))
                    for b in range(GT):
                        c = (q * GT + b) * 2
                        ins = a.activation(cut(ho, q, b), sums(q, b), ACT.Identity,
                                           bias=sc[:, c + 1:c + 2], scale=sc[:, c:c + 1])
                    ins.then_inc(act_done.sem, 1)
                    store(i, q)

                def x1_root(i, q):
                    act.wait_ge(row_var.sem, row_var.done(i * 2 + (GROUPS + q)))
                    roots(row_root, rsc, second(rmv, q, 1), q)

                def x1_norm(i, q):
                    act.wait_ge(x1_ready.sem, x1_ready.done(i * 2 + q))
                    act.wait_ge(T2_done.sem, T2_done.free(i * 2 + q))
                    for b in range(GT):
                        c = (q * GT + b) * 2
                        ins = a.activation(cut(zz, q, b), cut(x1, q, b), ACT.Relu,
                                           bias=rsc[:, c + 1:c + 2], scale=rsc[:, c:c + 1])
                    ins.then_inc(zz_ready.sem, 1)

                def turned_x1(i, q):
                    act.wait_ge(T2_done.sem, T2_done.done(i * 2 + q))
                    a.copy(zT[:, :], psT[:, :]).then_inc(zT_ready.sem, 1)

                def keep_v(i, q):
                    act.wait_ge(V_done.sem, V_done.done(i * 2 + q))
                    act.wait_ge(stored[q], i * 16 + (16 + 16 * ITERS * l))
                    a.copy(part(ho, q), psR[:, :]).then_inc(act_done.sem, 1)
                    store(i, q)

                def one(i, q):
                    this, before, before2, nx, nx2, rows3 = (shift(i, q, d) for d in (0, -1, -2, 1, 2, 3))
                    rows3 = rows3 if first else None
                    if before and not last:
                        keep_normed(*before)
                    if before2 and last:
                        turned_x1(*before2)
                    if nx:
                        keep_z(*nx)
                    if before2 and last:
                        keep_v(*before2)
                    if nx2:
                        turned(*nx2)
                        mlp(*nx2)
                    if this:
                        sum_roots(*this)
                    if rows3:
                        norm_root(*rows3)
                        norm(*rows3)
                    if last and before:
                        x1_root(*before)
                        x1_norm(*before)

                def body(i, lo):
                    for q in range(2):
                        one(i, q)

                bodies(act, body)

            for q in range(2):
                act.wait_ge(stored[q], 16 + 16 * ITERS * LAYERS)
            with act.Fori(0, ITERS) as i:
                for q in range(2):
                    n = i * 2 + q
                    act.wait_ge(M_done.sem, M_done.done(n))
                    for b in range(GT):
                        c = (q * GT + b) * 4 + 3
                        ins = a.activation(z[:, b * P:(b + 1) * P], psZ[:, b * P:(b + 1) * P], ACT.Copy,
                                           scale=stage_cols[:, c:c + 1])
                    ins.then_inc(m_ready.sem, 1)
                    act.wait_ge(C_done.sem, C_done.done(n))
                    act.wait_ge(staged, n + STAGED_BEFORE)
                    a.copy(part(ho, q), psT[:, :]).then_inc(c_ready.sem, 1)

        @block.tensor
        def _(pe):
            T = nc.tensor
            pe.wait_ge(credits_, 1)
            pe.wait_ge(loaded, 16 * 24)
            pe.wait_ge(seam_up, 1)
            T.transpose(psS[0:1, 0:P], seam[:, 0:1], ident[:, :])
            T.transpose(psS[0:1, P:2 * P], seam[:, 1:2], ident[:, :]).then_inc(seam_flat, 1)
            pe.wait_ge(seam_up, 2)
            T.matmul(psS[:, 2 * P:2 * P + 1], seam_row[0:1, 2 * P:3 * P], ident[0:1, 0:1], start=True, stop=True)
            T.matmul(psS[:, 2 * P + 1:2 * P + 2], seam_row[0:1, 3 * P:4 * P], ident[0:1, 0:1],
                     start=True, stop=True).then_inc(seam_down, 1)
            pe.wait_ge(turned_loaded, 16 * (GT + 1))
            for j in range(GT):
                ins = T.transpose(psR[:, j * TQ:(j + 1) * TQ], dis_t[:, j * P:(j + 1) * P], ident[0:TQ, 0:TQ])
            ins.then_inc(dis_turned, 1)

            pe.wait_ge(idx_ready, 1)
            for l in range(LAYERS):
                first, last = l == 0, l == LAYERS - 1
                LW = slice(l * D, (l + 1) * D)

                def turn(i, q):
                    n = G(l, i, q)
                    if first:
                        pe.wait_ge(g_ready.sem, g_ready.done(n))
                    else:
                        pe.wait_ge(gathered[q], i * (16 * GT) + (16 * GT * (ITERS * l + 1)))
                    pe.wait_ge(hT_ready.sem, hT_ready.done(n) - 1)
                    for b in range(GT):
                        ins = T.transpose(psT[:, b * P:(b + 1) * P], cut(gat, q, b), ident[:, :])
                    ins.then_inc(T_done.sem, 1)

                def mlp(i, q):
                    n = G(l, i, q)
                    pe.wait_ge(rT_ready.sem, rT_ready.done(n) - 1)
                    held = i * 16 + (16 * (ITERS * l + 1))
                    held = held if isinstance(held, int) else pe.to_reg(held)
                    pe.wait_ge(credits_, 1)
                    pe.wait_ge(attr_in[q], held)
                    T.matmul(psR[:, :], edge_w1[:, LW], part(attr, q), start=True, stop=True).then_inc(R_done.sem, 1)

                def per_edge(i, q, bs):
                    n = G(l, i, q)
                    if bs[0] == GT - 1:
                        pe.wait_ge(hT_ready.sem, hT_ready.done(n))
                        pe.wait_ge(rT_ready.sem, rT_ready.done(n))
                        pe.wait_ge(z_ready.sem, z_ready.done(n) - 1)
                        if not first:
                            pe.wait_ge(zr_ready.sem, zr_ready.done(G(l - 1, i, q)) - 1)
                    for b in bs:
                        zb = psZ[:, b * P:(b + 1) * P]
                        hb = zb if first else psH[:, b * P:(b + 1) * P]
                        T.matmul(hb, cut(hT, q, b), lin_w[:, LW], start=True, stop=not first)
                        ins = T.matmul(zb, cut(rT, q, b), edge_w2[:, LW], start=not first, stop=True)
                    if bs[-1] == 0:
                        ins.then_inc(Z_done.sem, 1)

                def tile_sum(i, q, s):
                    n, b = G(l, i, q), GT - 1 - s
                    if s == 0:
                        pe.wait_ge(z_ready.sem, z_ready.done(n))
                        pe.wait_ge(eq_ready.sem, eq_ready.done(n))
                        pe.wait_ge(rank3_in[q], i * 16 + (16 * (ITERS * l + 1)))
                        if last:
                            pe.wait_ge(U_free.sem, U_free.free(i * 2 + q))
                        else:
                            pe.wait_ge(act_done.sem, act_done.free(n))
                    if s >= 2:
                        pe.wait_ge(stat_done.sem, stat_done.done(n, s - 1))
                    T.matmul(sums(q, b), cut(eq, q, b), cut(z2, q, b), start=True, stop=False)

                def tile_carry(i, q, s):
                    n, b = G(l, i, q), GT - 1 - s
                    value = carried.done(n, s)
                    value = value if isinstance(value, int) else pe.to_reg(value)
                    pe.wait_ge(credits_, 1)
                    pe.wait_ge(carried.sem, value)
                    T.matmul(sums(q, b), rank3[:, (q * GT + b) * P:(q * GT + b + 1) * P], carry[:, LW],
                             start=False, stop=True).then_inc(U_done.sem, 1)

                def turn_x1(i, q):
                    pe.wait_ge(zz_ready.sem, zz_ready.done(i * 2 + q))
                    for b in range(GT):
                        ins = T.transpose(psT[:, b * P:(b + 1) * P], cut(zz, q, b), ident[:, :])
                    ins.then_inc(T2_done.sem, 1)

                def make_v(i, q):
                    pe.wait_ge(zT_ready.sem, zT_ready.done(i * 2 + q))
                    pe.wait_ge(act_done.sem, act_done.done(G(l, i, q)) - 1)
                    for b in range(GT):
                        ins = T.matmul(psR[:, b * P:(b + 1) * P], zT[:, b * P:(b + 1) * P], out_w[:, :],
                                       start=True, stop=True)
                    ins.then_inc(V_done.sem, 1)

                def one(i, q):
                    this, before2, nx, nx2 = (shift(i, q, d) for d in (0, -2, 1, 2))
                    before2 = before2 if last else None
                    if this:
                        tile_sum(*this, 0)
                        tile_carry(*this, 0)
                        tile_sum(*this, 1)
                    if before2:
                        if nx:
                            pe.wait_ge(hT_ready.sem, hT_ready.done(G(l, *nx)))
                        turn_x1(*before2)
                    if nx:
                        per_edge(*nx, (3, 2))
                    if this:
                        tile_carry(*this, 1)
                        tile_sum(*this, 2)
                    if nx:
                        per_edge(*nx, (1, 0))
                    if before2:
                        make_v(*before2)
                    if this:
                        tile_carry(*this, 2)
                        tile_sum(*this, 3)
                    if nx2:
                        turn(*nx2)
                        if before2:
                            pe.wait_ge(act_done.sem, act_done.done(G(l, *before2)))
                        mlp(*nx2)
                    if this:
                        tile_carry(*this, 3)

                def body(i, lo):
                    for q in range(2):
                        one(i, q)

                bodies(pe, body)

            with pe.Fori(0, ITERS) as i:
                for q in range(2):
                    n = i * 2 + q
                    pe.wait_ge(v_loaded[q], i * 48 + 48)
                    pe.wait_ge(eqs_ready.sem, eqs_ready.done(n))
                    pe.wait_ge(m_ready.sem, m_ready.done(n) - 1)
                    for b in range(GT):
                        ins = T.matmul(psZ[:, b * P:(b + 1) * P], cut(eq, q, b), cut(v_in, q, b), start=True, stop=True)
                    ins.then_inc(M_done.sem, 1)
                    pe.wait_ge(m_ready.sem, m_ready.done(n))
                    pe.wait_ge(c_ready.sem, c_ready.done(n) - 1)
                    for b in range(GT):
                        for k in range(GT):
                            s0 = (q * GT + k) * GE + b * P
                            ins = T.matmul(psT[:, b * P:(b + 1) * P], same_src[:, s0:s0 + P],
                                           z[:, k * P:(k + 1) * P], start=(k == 0), stop=(k == GT - 1))
                    ins.then_inc(C_done.sem, 1)


def kernel(x, src, dst, edge_attr_16, edge_weight, L0_gnn_lin_w, L0_gnn_edge_w1, L0_gnn_edge_b1, L0_gnn_edge_w2,
           L0_gnn_edge_b2, L0_gnn_bias, L0_gnn_ln_w, L0_gnn_ln_b, L1_gnn_W):
    import numpy as np
    import concourse.bacc as bacc
    from concourse import mybir as mb
    from concourse.bass_utils import run_bass_kernel_spmd

    def padded(a, fill):
        return np.concatenate([a, np.full((EP - E,) + a.shape[1:], fill, a.dtype)])

    def lay_a(a):
        return np.ascontiguousarray(a.reshape(TILES, P).T)

    def lay_b(a):
        return np.ascontiguousarray(a.reshape(P, TILES))

    src, dst = (np.asarray(a) for a in (src, dst))
    src_p, dst_p = padded(src, N), padded(dst, N)
    none = np.full((1,), -1, dst.dtype)
    prev, after = np.concatenate([none, dst_p[:-1]]), np.concatenate([dst_p[1:], none])
    pos = np.arange(EP, dtype=np.float32)
    tile0 = np.arange(TILES, dtype=np.float32).repeat(P) * P
    c = np.arange(GE)
    before = (c[None, None, :] < (c.reshape(GT, P).T)[:, :, None]).astype(np.float32).reshape(P, GT * GE)
    arrays = {
        "x": np.ascontiguousarray(x),
        "src_a": lay_a(src_p), "dst_a": lay_a(dst_p), "dst_a_prev": lay_a(prev),
        "ew_a": lay_a(padded(np.asarray(edge_weight), 0.0)),
        "dump_a": lay_a(np.tile(np.arange(GE, dtype=np.float32) + DUMP, GROUPS)),
        "dst_b": lay_b(dst_p), "dst_b_prev": lay_b(prev), "dst_b_next": lay_b(after),
        "pos_b": np.stack([lay_b(pos + 1), lay_b(tile0 + 1), lay_b(tile0 + P)]),
        "dst_row": dst_p[None, :], "src_row": src_p[None, :],
        "attr_t": np.ascontiguousarray(padded(np.asarray(edge_attr_16), 0.0).T),
        "lin_w": np.ascontiguousarray(L0_gnn_lin_w), "edge_w2": np.ascontiguousarray(L0_gnn_edge_w2),
        "edge_w1": np.concatenate([np.asarray(L0_gnn_edge_w1), np.asarray(L0_gnn_edge_b1)[:, None, :]], axis=1),
        "edge_b2": np.ascontiguousarray(L0_gnn_edge_b2), "bias": np.ascontiguousarray(L0_gnn_bias),
        "ln_w": np.ascontiguousarray(L0_gnn_ln_w), "ln_b": np.ascontiguousarray(L0_gnn_ln_b),
        "out_w": np.ascontiguousarray(L1_gnn_W),
        "ident": np.eye(P, dtype=np.float32), "before": before,
    }
    nc = bacc.Bacc("TRN2", target_bir_lowering=False, num_devices=1)
    t = {k: nc.dram_tensor(f"in_{k}", a.shape, mb.dt.from_np(a.dtype), kind="ExternalInput").ap()
         for k, a in arrays.items()}
    t["out"] = nc.dram_tensor("out", (ROWS_OUT, D), mb.dt.float32, kind="ExternalOutput").ap()
    gnn(nc, t)
    r = run_bass_kernel_spmd(nc, [{f"in_{k}": a for k, a in arrays.items()}], core_ids=[0])
    return r.results[0]["out"][:N]
```

```python
import concourse.bass as bass
from concourse import mybir
from contextlib import ExitStack

N = 100000
E = 50000
D = 128
DE = 16
LAYERS = 3
P = 128
GT = 4
GROUPS = -(-E // (P * GT))
ITERS = GROUPS // 2
TILES = GROUPS * GT
EP = TILES * P
GE = GT * P
DUMP = N + 1
ROWS_OUT = DUMP + GE
SKIP = 2 * N
LN_EPS = 1e-5
FAR = 2.0 * EP
XP, CHUNKS = 125, GROUPS + 2
CR = N // (XP * CHUNKS)
assert XP * CHUNKS * CR == N
CW = CR * D
TQ = TILES // GT
STAGED_BEFORE = GROUPS * (2 + LAYERS)


class Count:

    def __init__(self, sem, per=1, credit=None):
        self.sem, self.per = sem, per
        self.credit = 2 * per if credit is None else credit

    def done(self, n, k=None):
        return n * self.per + (self.credit + (self.per if k is None else k))

    def free(self, n):
        return n * self.per + (self.credit - self.per)


def gnn(nc, t):
    f32, i32 = mybir.dt.float32, mybir.dt.int32
    ALU, ACT = mybir.AluOpType, mybir.ActivationFunctionType
    ctx = ExitStack()
    with ctx:
        def sb(name, shape, dt=f32):
            return ctx.enter_context(nc.sbuf_tensor(name, shape, dt))

        def ps(name):
            return ctx.enter_context(nc.psum_tensor(name, [P, GE], f32))

        def sem(name):
            return ctx.enter_context(nc.semaphore(name))

        ident = sb("ident", [P, P])
        lin_w = sb("lin_w", [P, LAYERS * D])
        edge_w2 = sb("edge_w2", [P, LAYERS * D])
        edge_w1 = sb("edge_w1", [DE + 1, LAYERS * D])
        out_w = sb("out_w", [P, D])
        ln_w = sb("ln_w", [P, LAYERS * D])
        ln_b = sb("ln_b", [P, LAYERS * D])
        last_bias = sb("last_bias", [P, D])
        carry = sb("carry", [3, LAYERS * D])
        zeros = sb("zeros", [P, 2000])
        dst_b = sb("dst_b", [P, TILES], i32)
        dst_b_prev = sb("dst_b_prev", [P, TILES], i32)
        dst_b_next = sb("dst_b_next", [P, TILES], i32)
        pos_b = sb("pos_b", [P, 3 * TILES])
        is_head_b = sb("is_head_b", [P, TILES])
        is_tail_b = sb("is_tail_b", [P, TILES])
        head_b = sb("head_b", [P, TILES])
        tail_b = sb("tail_b", [P, TILES])
        deg_b = sb("deg_b", [P, TILES])
        dis_b = sb("dis_b", [P, TILES])
        root_b = sb("root_b", [P, TILES])
        goes_on_b = sb("goes_on_b", [P, TILES])
        bias_row_b = sb("bias_row_b", [P, TILES])
        b2_row_b = sb("b2_row_b", [P, TILES])
        tmp_b = sb("tmp_b", [P, TILES])
        node_idx_b = sb("node_idx_b", [P, TILES], i32)
        node_row_b = sb("node_row_b", [P, 2 * TILES])
        seam = sb("seam", [P, 4])
        seam_row = sb("seam_row", [1, 4 * P])
        src_a = sb("src_a", [P, TILES], i32)
        dst_a = sb("dst_a", [P, TILES], i32)
        dst_a_prev = sb("dst_a_prev", [P, TILES], i32)
        dump_a = sb("dump_a", [P, TILES])
        ew_a = sb("ew_a", [P, TILES])
        is_head_a = is_tail_b
        tmp_a = tmp_b
        src_f = sb("src_f", [P, TILES])
        cols = sb("cols", [P, TILES * 4])
        cols_out = sb("cols_out", [P, TILES * 4])
        own = sb("own", [P, 2 * TILES])
        src_row_idx = sb("src_row_idx", [P, TILES], i32)
        x1_idx = sb("x1_idx", [P, TILES], i32)
        add_idx = sb("add_idx", [P, TILES], i32)
        earlier = sb("earlier", [P, TILES])
        before = sb("before", [P, GT * GE])
        dis_t = sb("dis_t", [TQ, GT * P])
        first_head = sb("first_head", [TQ, GT])
        first_idx = sb("first_idx", [TQ, GT], i32)
        first_v = sb("first_v", [TQ, GT * D])
        attr_s = sb("attr_s", [P, EP // 8])
        root_s = sb("root_s", [P, EP // 8])
        y, ho, x1, v_in, zz = (root_s[:, k * 2 * GE:(k + 1) * 2 * GE] for k in range(5))
        x_normed = y
        zT = root_s[:, 10 * GE:11 * GE]
        xin = sb("xin", [P, 2 * CW])
        xout = sb("xout", [P, 2 * CW])
        hT, rT = (xin[:, k * 2 * GE:(k + 1) * 2 * GE] for k in range(2))
        z2 = sb("z2", [P, 2 * GE])
        base = sb("base", [P, D])
        stage_idx = sb("stage_idx", [P, 2 * GT], i32)
        stage_idx2 = sb("stage_idx2", [P, 2 * GT], i32)
        stage_idx3 = sb("stage_idx3", [P, 2 * GT], i32)
        stage_row = sb("stage_row", [P, 2 * 2 * GT])
        stage_cols = sb("stage_cols", [P, 2 * 4 * GT])
        gat = sb("gat", [P, 2 * GE])
        rows = sb("rows", [P, 2 * GE], i32)
        rows_src = sb("rows_src", [P, 2 * GE], i32)
        attr = sb("attr", [DE + 1, 2 * GE])
        rank3 = sb("rank3", [3, 2 * GE])
        eq = sb("eq", [P, 2 * GE])
        same_src = attr_s
        z = sb("z", [P, GE])
        xd = sb("xd", [P, 2 * GE])
        ln_cols = sb("ln_cols", [P, 2 * LAYERS])
        stats = sb("stats", [P, GT * 6])
        rstats = sb("rstats", [P, GT * 6])
        rmv = sb("rmv", [P, 2 * GT * 2])
        rsc = sb("rsc", [P, 2 * GT * 2])
        mv = sb("mv", [P, 2 * GT * 2])
        sc = sb("sc", [P, 2 * GT * 2])
        eps = sb("eps", [P, 1])
        junk = root_s[:, 0:GT * GE]

        psT, psR, psZ = (ps(n) for n in ("psT", "psR", "psZ"))
        psH = ps("psH")
        psS = psZ
        psU = [[ps("psU00"), ps("psU01")], [ps("psU10"), ps("psU11")]]

        def sums(q, b, rows=P):
            return psU[q][b % 2][0:rows, (b // 2) * P:(b // 2 + 1) * P]

        def dram(name, shape, dt=f32):
            return nc.dram_tensor(name, shape, dt, kind="Internal").ap()

        node_tab = dram("node_tab", (N, 2))
        attr_d = dram("attr_d", (DE + 1, EP))
        rank3_d = dram("rank3_d", (3, EP))
        dis_d = dram("dis_d", (EP,))
        head_d = dram("head_d", (EP,))
        h_tab = [dram(f"h_tab{l}", (EP + 1, D)) for l in range(2)]
        x_dst = dram("x_dst", [EP, D])
        v_tab = dram("v_tab", (EP + 1, D))
        out = t["out"]

        credits_ = sem("credits_")
        loaded = sem("loaded")
        zeroed = sem("zeroed")
        v_zeroed = sem("v_zeroed")
        srcs_ready = sem("srcs_ready")
        xd_stored = [sem("xd_stored0"), sem("xd_stored1")]
        xd_loaded = [sem("xd_loaded0"), sem("xd_loaded1")]
        dve_step = sem("dve_step")
        pool_step = sem("pool_step")
        seam_up = sem("seam_up")
        seam_flat = sem("seam_flat")
        seam_down = sem("seam_down")
        edge_ready = sem("edge_ready")
        edge_stored = sem("edge_stored")
        attr_loaded = sem("attr_loaded")
        attr_scaled = sem("attr_scaled")
        attr_stored = sem("attr_stored")
        turned_loaded = sem("turned_loaded")
        dis_turned = sem("dis_turned")
        tab_zeroed = [sem("tab_zeroed0"), sem("tab_zeroed1")]
        tab_free = [sem("tab_free0"), sem("tab_free1")]
        own_in = [sem("own_in0"), sem("own_in1")]
        own_kept = Count(sem("own_kept"))
        x_in = [sem("x_in0"), sem("x_in1")]
        x_based = Count(sem("x_based"))
        base_out = [sem("base_out0"), sem("base_out1")]
        dup_rows = [sem("dup_rows0"), sem("dup_rows1")]
        dup_done = Count(sem("dup_done"))
        idx_ready = sem("idx_ready")
        staged = sem("staged")
        gathered = [sem("gathered0"), sem("gathered1")]
        xd_in = [sem("xd_in0"), sem("xd_in1")]
        x1_out = [sem("x1_out0"), sem("x1_out1")]
        rows_in = [sem("rows_in0"), sem("rows_in1")]
        attr_in = [sem("attr_in0"), sem("attr_in1")]
        rank3_in = [sem("rank3_in0"), sem("rank3_in1")]
        stored = [sem("stored0"), sem("stored1")]
        var_ready = sem("var_ready")
        root_ready = sem("root_ready")
        sum_var = Count(sem("sum_var"))
        sum_root = Count(sem("sum_root"))
        row_var = Count(sem("row_var"))
        row_root = Count(sem("row_root"))
        normed = Count(sem("normed"))
        g_ready = Count(sem("g_ready"))
        T_done = Count(sem("T_done"))
        hT_ready = Count(sem("hT_ready"))
        R_done = Count(sem("R_done"))
        rT_ready = Count(sem("rT_ready"))
        Z_done = Count(sem("Z_done"))
        zr_ready = Count(sem("zr_ready"))
        z_ready = Count(sem("z_ready"))
        eq_ready = Count(sem("eq_ready"))
        U_done = Count(sem("U_done"), GT)
        carried = Count(sem("carried"), GT)
        stat_done = Count(sem("stat_done"), GT)
        U_free = Count(sem("U_free"))
        y_ready = Count(sem("y_ready"))
        act_done = Count(sem("act_done"))
        h_ready = Count(sem("h_ready"))
        x1_ready = Count(sem("x1_ready"))
        zz_ready = Count(sem("zz_ready"))
        T2_done = Count(sem("T2_done"))
        zT_ready = Count(sem("zT_ready"))
        V_done = Count(sem("V_done"))
        firsts_in = sem("firsts_in")
        firsts_out = sem("firsts_out")
        added = sem("added")
        v_loaded = [sem("v_loaded0"), sem("v_loaded1")]
        eqs_ready = Count(sem("eqs_ready"))
        M_done = Count(sem("M_done"))
        m_ready = Count(sem("m_ready"))
        C_done = Count(sem("C_done"))
        c_ready = Count(sem("c_ready"))

        def G(l, i, q):
            return i * 2 + (GROUPS * l + q)

        def cut(buf, q, b, w=P):
            return buf[:, (q * GT + b) * w:(q * GT + b + 1) * w]

        def part(buf, q, w=GE):
            return buf[:, q * w:(q + 1) * w]

        def shift(i, q, d):
            if isinstance(i, int) and not 0 <= i * 2 + q + d < GROUPS:
                return None
            return i + (q + d) // 2, (q + d) % 2

        def bodies(engine, body, last):
            lo = 2 if last else 1
            for i in range(-2, lo):
                body(i, None)
            with engine.Fori(lo, ITERS - 2) as i:
                body(i, lo)
            for i in range(ITERS - 2, ITERS + lo):
                body(i, None)

        block = ctx.enter_context(nc.Block())

        @block.sync
        def _(sp):
            def load(dst, src):
                sp.dma_start(dst, src).then_inc(loaded, 16)

            load(dst_b[:, :], t["dst_b"])
            load(dst_b_prev[:, :], t["dst_b_prev"])
            load(dst_b_next[:, :], t["dst_b_next"])
            for k in range(3):
                load(pos_b[:, k * TILES:(k + 1) * TILES], t["pos_b"][k])
            load(ident[:, :], t["ident"])
            load(src_a[:, :], t["src_a"])
            load(dst_a[:, :], t["dst_a"])
            load(dst_a_prev[:, :], t["dst_a_prev"])
            load(dump_a[:, :], t["dump_a"])
            load(ew_a[:, :], t["ew_a"])
            load(before[:, :], t["before"])
            load(lin_w[:, :].rearrange("p (l d) -> p l d", l=LAYERS), t["lin_w"].rearrange("l p d -> p l d"))
            load(edge_w2[:, :].rearrange("p (l d) -> p l d", l=LAYERS), t["edge_w2"].rearrange("l p d -> p l d"))
            load(edge_w1[:, :].rearrange("p (l d) -> p l d", l=LAYERS), t["edge_w1"].rearrange("l p d -> p l d"))
            load(out_w[:, :], t["out_w"])
            load(ln_w[:, :], t["ln_w"].rearrange("(o l) d -> o (l d)", o=1).broadcast_to([P, LAYERS * D]))
            load(ln_b[:, :], t["ln_b"].rearrange("(o l) d -> o (l d)", o=1).broadcast_to([P, LAYERS * D]))
            with nc.allow_non_contiguous_dma(reason="six columns"):
                load(ln_cols[:, 0:LAYERS], t["ln_w"].rearrange("l d -> d l"))
                load(ln_cols[:, LAYERS:2 * LAYERS], t["ln_b"].rearrange("l d -> d l"))
            load(last_bias[:, :], t["bias"][LAYERS - 1:LAYERS, :].broadcast_to([P, D]))
            load(carry[1:2, :], t["bias"].rearrange("(o l) d -> o (l d)", o=1))
            load(carry[2:3, :], t["edge_b2"].rearrange("(o l) d -> o (l d)", o=1))
            sp.dma_start(attr_s[:, :], t["attr_t"].rearrange("j (c r) -> (j c) r", c=8)).then_inc(attr_loaded, 16)

            sp.wait_ge(zeroed, 1)
            half = N // 2
            for q in range(2):
                sp.dma_start(node_tab[q * half:(q + 1) * half, :].rearrange("(p r) c -> p (r c)", p=50),
                             zeros[0:50, 0:2000]).then_inc(tab_zeroed[q], 16)
            for l in range(2):
                sp.dma_start(h_tab[l][0:1, :], zeros[0:1, 0:D]).then_inc(stored[l], 16)

            sp.dma_start(v_tab[0:1, :], zeros[0:1, 0:D]).then_inc(v_zeroed, 16)

            sp.wait_ge(edge_ready, 1)
            for dst, src in ((rank3_d[0], goes_on_b), (rank3_d[1], bias_row_b), (rank3_d[2], b2_row_b),
                             (attr_d[DE], root_b), (dis_d, dis_b), (head_d, head_b)):
                sp.dma_start(dst.rearrange("(p c) -> p c", c=TILES), src[:, :]).then_inc(edge_stored, 16)
            sp.wait_ge(edge_stored, 16 * 6)
            for j in range(DE):
                sp.dma_start(root_s[j * 8:(j + 1) * 8, :],
                             attr_d[DE].rearrange("(c r) -> c r", c=8)).then_inc(attr_loaded, 16)
            sp.dma_start(dis_t[:, :].rearrange("t (j p) -> t j p", j=GT),
                         dis_d.rearrange("(j t p) -> t j p", j=GT, p=P)).then_inc(turned_loaded, 16)
            with nc.allow_non_contiguous_dma(reason="one head row for each tile"):
                for j in range(GT):
                    sp.dma_start(first_head[:, j:j + 1],
                                 head_d.rearrange("(j t p) -> j t p", j=GT, p=P)[j, :, 0:1]).then_inc(turned_loaded, 16)

            xv = t["x"].rearrange("(p r) d -> p (r d)", p=XP)
            ov = out[0:N, :].rearrange("(p r) d -> p (r d)", p=XP)

            def load_x(c, q):
                sp.dma_start(part(xin, q, CW)[0:XP, :], xv[:, bass.ds(c * CW, CW)]).then_inc(x_in[q], 16)

            def store_based(c, q):
                sp.dma_start(ov[:, bass.ds(c * CW, CW)], part(xout, q, CW)[0:XP, :]).then_inc(base_out[q], 16)

            for q in range(2):
                load_x(q, q)
            with sp.Fori(0, ITERS) as i:
                for q in range(2):
                    n = i * 2 + q
                    sp.wait_ge(x_based.sem, x_based.done(n))
                    load_x(n + 2, q)
                    store_based(n, q)
                    sp.wait_ge(dup_done.sem, dup_done.free(n))
                    sp.dma_start(part(rows_src, q), t["src_row"][0:1, bass.ds(n * GE, GE)]
                                 .broadcast_to([P, GE])).then_inc(dup_rows[q], 16)
            for q in range(2):
                sp.wait_ge(x_based.sem, x_based.done(CHUNKS - 2 + q))
                store_based(CHUNKS - 2 + q, q)
            sp.dma_start(out[DUMP:ROWS_OUT, :].rearrange("(p r) d -> p (r d)", p=P),
                         zeros[:, 0:GT * D]).then_inc(edge_stored, 16)
            sp.dma_start(out[N:N + 1, :], zeros[0:1, 0:D]).then_inc(edge_stored, 16)

            sp.wait_ge(attr_scaled, 1)
            sp.dma_start(attr_d[0:DE].rearrange("j (c r) -> (j c) r", c=8), attr_s[:, :]).then_inc(attr_stored, 16)
            sp.wait_ge(attr_stored, 16)

            def load_attr(l, i, q):
                sp.wait_ge(R_done.sem, R_done.free(G(l, i, q)))
                sp.dma_start(part(attr, q), attr_d[:, bass.ds(i * (-2 * GE) + (GROUPS - 1 - q) * GE, GE)]
                             ).then_inc(attr_in[q], 16)

            def load_rows(l, i, q):
                at = i * (-2 * GE) + (GROUPS - 1 - q) * GE
                n = G(l, i, q)
                sp.wait_ge(eq_ready.sem, eq_ready.free(n))
                sp.dma_start(part(rows, q), t["dst_row"][0:1, bass.ds(at, GE)]
                             .broadcast_to([P, GE])).then_inc(rows_in[q], 16)
                sp.wait_ge(U_done.sem, U_done.free(n))
                sp.dma_start(part(rank3, q), rank3_d[:, bass.ds(at, GE)]).then_inc(rank3_in[q], 16)

            def x_dst_rows(i, q):
                return x_dst.rearrange("(c p) d -> p c d", p=P)[
                    :, bass.ds(i * (-2 * GT) + (GROUPS - 1 - q) * GT, GT), :]

            def x_dst_set(q):
                return part(xd, q).rearrange("p (b d) -> p b d", b=GT)

            def keep_x_dst(l, i, q):
                if l == LAYERS - 2:
                    sp.wait_ge(xd_in[q], i * (16 * GT) + 16 * GT)
                    sp.dma_start(x_dst_rows(i, q), x_dst_set(q)).then_inc(xd_stored[q], 16)

            def get_x_dst(l, i, q):
                if l == LAYERS - 1:
                    sp.wait_ge(x1_ready.sem, x1_ready.free(i * 2 + q))
                    sp.dma_start(x_dst_set(q), x_dst_rows(i, q)).then_inc(xd_loaded[q], 16)

            for l in range(LAYERS):
                if l == LAYERS - 1:
                    for q in range(2):
                        sp.wait_ge(xd_stored[q], 16 * ITERS)
                load_attr(l, 0, 0)
                load_attr(l, 0, 1)
                load_rows(l, 0, 0)
                keep_x_dst(l, 0, 0)
                load_attr(l, 1, 0)
                load_rows(l, 0, 1)
                keep_x_dst(l, 0, 1)
                get_x_dst(l, 0, 0)
                with sp.Fori(1, ITERS - 1) as i:
                    load_attr(l, i, 1)
                    keep_x_dst(l, i, 0)
                    load_rows(l, i, 0)
                    get_x_dst(l, i - 1, 1)
                    load_attr(l, i + 1, 0)
                    keep_x_dst(l, i, 1)
                    load_rows(l, i, 1)
                    get_x_dst(l, i, 0)
                load_attr(l, ITERS - 1, 1)
                keep_x_dst(l, ITERS - 1, 0)
                load_rows(l, ITERS - 1, 0)
                get_x_dst(l, ITERS - 2, 1)
                keep_x_dst(l, ITERS - 1, 1)
                load_rows(l, ITERS - 1, 1)
                get_x_dst(l, ITERS - 1, 0)
                get_x_dst(l, ITERS - 1, 1)

            sp.wait_ge(firsts_in, 16 * GT)
            for j in range(GT):
                sp.dma_start(v_tab[1:EP + 1, :].rearrange("(j t p) d -> j t p d", j=GT, p=P)[j, :, 0, :],
                             first_v[:, j * D:(j + 1) * D]).then_inc(firsts_out, 16)
            sp.wait_ge(firsts_out, 16 * GT)
            with sp.Fori(0, ITERS) as i:
                for q in range(2):
                    n = i * 2 + q
                    at = n * GE
                    sp.wait_ge(eqs_ready.sem, eqs_ready.free(n))
                    sp.wait_ge(M_done.sem, M_done.free(n))
                    sp.dma_start(part(rows, q), t["dst_row"][0:1, bass.ds(at, GE)]
                                 .broadcast_to([P, GE])).then_inc(v_loaded[q], 16)
                    sp.dma_start(part(rows_src, q), t["src_row"][0:1, bass.ds(at, GE)]
                                 .broadcast_to([P, GE])).then_inc(v_loaded[q], 16)
                    sp.dma_start(part(v_in, q).rearrange("p (b d) -> p b d", b=GT),
                                 v_tab[1:EP + 1, :].rearrange("(n p) d -> p n d", p=P)[:, bass.ds(n * GT, GT), :]
                                 ).then_inc(v_loaded[q], 16)

        @block.gpsimd
        def _(pool):
            steps = [0]

            def hold(s, value):
                if isinstance(value, int):
                    pool.wait_ge(s, value)
                    return
                r = pool.to_reg(value)
                pool.wait_ge(credits_, 1)
                pool.wait_ge(s, r)

            def peeled(body):
                body(0, True)
                with pool.Fori(1, ITERS) as i:
                    body(i, False)

            pool.memset(zeros[:, :], 0.0).then_inc(zeroed, 1)
            pool.memset(gat[:, :], 0.0)
            pool.memset(xd[:, :], 0.0)
            pool.memset(stage_row[:, :], 0.0)
            pool.memset(own[:, :], 0.0)
            pool.memset(carry[0:1, :], 0.0).then_inc(pool_step, 1)
            node_bound = pool.to_reg(N - 1)
            tab_bound = pool.to_reg(EP)
            out_bound = pool.to_reg(ROWS_OUT - 1)
            pool.wait_ge(pool_step, 1)

            pool.wait_ge(edge_ready, 1)
            for q in range(2):
                pool.wait_ge(tab_zeroed[q], 16)

            def fill_node_tab(i, first):
                for q in range(2):
                    if not first:
                        hold(tab_free[q], i * (16 * GT))
                    pool.tensor_copy(part(stage_idx, q, GT), node_idx_b[:, bass.ds((i * 2 + q) * GT, GT)])
                    pool.tensor_copy(part(stage_row, q, 2 * GT),
                                     node_row_b[:, bass.ds((i * 2 + q) * (2 * GT), 2 * GT)]).then_inc(staged, 1)
                    hold(staged, i * 2 + (q + 1))
                    for b in range(GT):
                        pool.indirect_dma_start(
                            node_tab[:, :], bass.IndirectOffsetOnAxis(ap=cut(stage_idx, q, b, 1), axis=0),
                            cut(stage_row, q, b, 2), None, bounds_check=node_bound,
                            oob_is_err=False).then_inc(tab_free[q], 16)

            peeled(fill_node_tab)
            for q in range(2):
                pool.wait_ge(tab_free[q], 16 * GT * ITERS)

            steps[0] = 2 * ITERS

            for l in range(LAYERS):
                last = l == LAYERS - 1
                if l:
                    pool.wait_ge(srcs_ready, 1)
                    for q in range(2):
                        pool.wait_ge(stored[q], 16 + 16 * ITERS * l)
                if last:
                    for q in range(2):
                        pool.wait_ge(base_out[q], 16 * (CHUNKS // 2))
                    pool.wait_ge(edge_stored, 16 * 8)
                idx = src_a if l == 0 else src_row_idx
                table, bound = (t["x"], node_bound) if l == 0 else (h_tab[l - 1], tab_bound)

                def at(i, q):
                    return bass.ds(i * (-2 * GT) + (GROUPS - 1 - q) * GT, GT)

                def fetch(i, q, value):
                    read = T_done if l else g_ready
                    hold(read.sem, read.free(G(l, i, q)))
                    if l == 0:
                        hold(own_kept.sem, own_kept.free(i * 2 + q))
                    if l == LAYERS - 2:
                        if shift(i, q, -2):
                            hold(xd_stored[q], i * 16)
                        pool.tensor_copy(part(stage_idx2, q, GT), dst_a[:, at(i, q)])
                    pool.tensor_copy(part(stage_idx, q, GT), idx[:, at(i, q)]).then_inc(staged, 1)
                    hold(staged, value)
                    for b in reversed(range(GT)):
                        pool.indirect_dma_start(
                            cut(gat, q, b), None, table[:, :],
                            bass.IndirectOffsetOnAxis(ap=cut(stage_idx, q, b, 1), axis=0),
                            bounds_check=bound, oob_is_err=False).then_inc(gathered[q], 16)
                    if l == 0:
                        for b in range(GT):
                            pool.indirect_dma_start(
                                cut(stage_row, q, b, 2), None, node_tab[:, :],
                                bass.IndirectOffsetOnAxis(ap=cut(stage_idx, q, b, 1), axis=0),
                                bounds_check=node_bound, oob_is_err=False).then_inc(own_in[q], 16)
                    if l == LAYERS - 2:
                        for b in range(GT):
                            pool.indirect_dma_start(
                                cut(xd, q, b), None, t["x"][:, :],
                                bass.IndirectOffsetOnAxis(ap=cut(stage_idx2, q, b, 1), axis=0),
                                bounds_check=node_bound, oob_is_err=False).then_inc(xd_in[q], 16)

                def send_x1(i, q, value):
                    hold(x1_ready.sem, x1_ready.done(i * 2 + q))
                    pool.tensor_copy(part(stage_idx3, q, GT), x1_idx[:, at(i, q)]).then_inc(staged, 1)
                    hold(staged, value)
                    for b in range(GT):
                        pool.indirect_dma_start(
                            out[:, :], bass.IndirectOffsetOnAxis(ap=cut(stage_idx3, q, b, 1), axis=0),
                            cut(x1, q, b), None, bounds_check=node_bound,
                            oob_is_err=False).then_inc(x1_out[q], 16)

                if not last:
                    for q in range(2):
                        fetch(0, q, steps[0] + q + 1)
                    with pool.Fori(1, ITERS - 1) as i:
                        for q in range(2):
                            fetch(i, q, i * 2 + (steps[0] + q + 1))
                    for q in range(2):
                        fetch(ITERS - 1, q, steps[0] + GROUPS - 1 + q)
                    steps[0] += GROUPS
                    continue
                for n in range(5):
                    fetch(n // 2, n % 2, steps[0] + n + 1)
                fetch(2, 1, steps[0] + 6)
                send_x1(0, 0, steps[0] + 7)
                steps[0] += 7
                with pool.Fori(3, ITERS) as i:
                    value = i * 4 + (steps[0] - 12)
                    fetch(i, 0, value + 1)
                    send_x1(i - 3, 1, value + 2)
                    fetch(i, 1, value + 3)
                    send_x1(i - 2, 0, value + 4)
                steps[0] += 4 * (ITERS - 3)
                for n in range(GROUPS - 5, GROUPS):
                    steps[0] += 1
                    send_x1(n // 2, n % 2, steps[0])

            for q in range(2):
                pool.wait_ge(stored[q], 16 + 16 * ITERS * LAYERS)
                pool.wait_ge(x1_out[q], 16 * GT * ITERS)
            pool.wait_ge(v_zeroed, 16)
            for j in range(GT):
                pool.indirect_dma_start(
                    first_v[:, j * D:(j + 1) * D], None, v_tab[:, :],
                    bass.IndirectOffsetOnAxis(ap=first_idx[:, j:j + 1], axis=0),
                    bounds_check=tab_bound, oob_is_err=False).then_inc(firsts_in, 16)

            assert steps[0] == STAGED_BEFORE, steps[0]

            def stage_add(n, q):
                pool.tensor_copy(part(stage_idx, q, GT), add_idx[:, bass.ds(n * GT, GT)]).then_inc(staged, 1)

            def add_message(i, q, next_too=True):
                n = i * 2 + q
                hold(c_ready.sem, c_ready.done(n))
                hold(staged, n + (STAGED_BEFORE + 1))
                if not isinstance(n, int) or n:
                    hold(added, n * (16 * GT))
                for b in range(GT):
                    pool.indirect_dma_start(
                        out[:, :], bass.IndirectOffsetOnAxis(ap=cut(stage_idx, q, b, 1), axis=0),
                        cut(ho, q, b), None, bounds_check=out_bound,
                        oob_is_err=True, compute_op=ALU.add).then_inc(added, 16)
                if next_too:
                    stage_add(n + 1, 1 - q)

            stage_add(0, 0)
            for q in range(2):
                add_message(0, q)
            with pool.Fori(1, ITERS - 1) as i:
                for q in range(2):
                    add_message(i, q)
            add_message(ITERS - 1, 0)
            add_message(ITERS - 1, 1, False)
            pool.wait_ge(added, 16 * GT * GROUPS)

        @block.vector
        def _(dve):
            v = nc.vector
            chain = [0]

            def link(ins):
                chain[0] += 1
                ins.then_inc(dve_step, 1)
                dve.wait_ge(dve_step, chain[0])

            for c in (sum_var, sum_root, row_var, row_root, own_kept, x_based, dup_done, normed, g_ready, T_done, hT_ready, R_done, rT_ready,
                      Z_done, zr_ready, z_ready, eq_ready, U_done, carried, stat_done, U_free, y_ready, act_done, h_ready,
                      x1_ready, zz_ready, T2_done, zT_ready, V_done, eqs_ready, M_done, m_ready, C_done,
                      c_ready):
                dve.sem_inc(c.sem, c.credit)
            dve.sem_inc(credits_, 1)
            v.memset(eps[:, :], LN_EPS)

            dve.wait_ge(loaded, 16 * 24)
            pos1, tile0, tile1 = (pos_b[:, k * TILES:(k + 1) * TILES] for k in range(3))
            v.tensor_tensor(is_head_b[:, :], dst_b[:, :], dst_b_prev[:, :], ALU.not_equal)
            link(v.tensor_tensor(is_tail_b[:, :], dst_b[:, :], dst_b_next[:, :], ALU.not_equal))
            v.tensor_tensor(tmp_b[:, :], is_head_b[:, :], pos1, ALU.mult)
            link(v.scalar_tensor_tensor(tail_b[:, :], pos1, -FAR, is_tail_b[:, :], ALU.add, ALU.mult))
            link(v.tensor_scalar(tail_b[:, :], tail_b[:, :], FAR, None, ALU.add))
            v.tensor_tensor_scan(head_b[:, :], tmp_b[:, :], tmp_b[:, :], 0.0, ALU.max, ALU.max)
            link(v.tensor_tensor_scan(tail_b[:, ::-1], tail_b[:, ::-1], tail_b[:, ::-1], FAR, ALU.min, ALU.min))
            v.tensor_copy(seam[:, 0:1], head_b[:, TILES - 1:TILES])
            v.tensor_copy(seam[:, 1:2], tail_b[:, 0:1]).then_inc(seam_up, 1)
            dve.wait_ge(seam_flat, 1)
            v.tensor_copy(seam_row[0:1, 0:P], psS[0:1, 0:P])
            link(v.tensor_copy(seam_row[0:1, P:2 * P], psS[0:1, P:2 * P]))
            v.memset(seam_row[0:1, 2 * P:2 * P + 1], 0.0)
            v.memset(seam_row[0:1, 4 * P - 1:4 * P], FAR)
            v.tensor_tensor_scan(seam_row[0:1, 2 * P + 1:3 * P], seam_row[0:1, 0:P - 1], seam_row[0:1, 0:P - 1],
                                 0.0, ALU.max, ALU.max)
            v.tensor_tensor_scan(seam_row[0:1, 3 * P:4 * P - 1][:, ::-1], seam_row[0:1, P + 1:2 * P][:, ::-1],
                                 seam_row[0:1, P + 1:2 * P][:, ::-1], FAR, ALU.min, ALU.min).then_inc(seam_up, 1)
            dve.wait_ge(seam_down, 1)
            link(v.tensor_copy(seam[:, 2:4], psS[:, 2 * P:2 * P + 2]))
            v.tensor_scalar(head_b[:, :], head_b[:, :], seam[:, 2:3], None, ALU.max)
            link(v.tensor_scalar(tail_b[:, :], tail_b[:, :], seam[:, 3:4], None, ALU.min))
            link(v.scalar_tensor_tensor(deg_b[:, :], tail_b[:, :], 1.0, head_b[:, :], ALU.add, ALU.subtract))
            v.engine_nop().then_inc(var_ready, 1)
            dve.wait_ge(root_ready, 1)
            link(v.reciprocal(dis_b[:, :], root_b[:, :]))
            v.tensor_tensor(goes_on_b[:, :], tail_b[:, :], tile1, ALU.is_gt)
            v.tensor_tensor(tmp_b[:, :], head_b[:, :], tile0, ALU.max)
            link(v.tensor_tensor(b2_row_b[:, :], tail_b[:, :], tile1, ALU.min))
            link(v.scalar_tensor_tensor(b2_row_b[:, :], b2_row_b[:, :], 1.0, tmp_b[:, :], ALU.add, ALU.subtract))
            v.tensor_tensor(b2_row_b[:, :], b2_row_b[:, :], root_b[:, :], ALU.mult)
            link(v.tensor_scalar(bias_row_b[:, :], goes_on_b[:, :], -1.0, 1.0, ALU.mult, ALU.add))
            v.tensor_tensor(bias_row_b[:, :], bias_row_b[:, :], root_b[:, :], ALU.mult)
            row2 = node_row_b[:, :].rearrange("p (c k) -> p c k", k=2)
            v.tensor_copy(row2[:, :, 0], pos1)
            v.tensor_copy(row2[:, :, 1], dis_b[:, :])
            link(v.scalar_tensor_tensor(tmp_b[:, :], dst_b[:, :], -float(SKIP), is_head_b[:, :], ALU.add, ALU.mult))
            v.tensor_scalar(node_idx_b[:, :], tmp_b[:, :], float(SKIP), None, ALU.add).then_inc(edge_ready, 1)

            cc = cols[:, :].rearrange("p (c k) -> p c k", k=4)
            co = cols_out[:, :].rearrange("p (c k) -> p c k", k=4)
            v.tensor_copy(cc[:, :, 0], dst_a[:, :])
            v.memset(cc[:, :, 3], 0.0)
            v.tensor_copy(co[:, :, 0], dst_a[:, :])
            v.tensor_copy(co[:, :, 2], src_a[:, :])
            v.tensor_copy(src_f[:, :], src_a[:, :])
            v.tensor_copy(co[:, :, 3], ew_a[:, :])
            link(v.tensor_tensor(is_head_a[:, :], dst_a[:, :], dst_a_prev[:, :], ALU.not_equal))
            link(v.tensor_copy(co[:, :, 1], is_head_a[:, :]))
            v.memset(co[0:1, :, 1], 1.0)
            link(v.scalar_tensor_tensor(tmp_a[:, :], dst_a[:, :], -float(SKIP), is_head_a[:, :], ALU.add, ALU.mult))
            link(v.tensor_scalar(x1_idx[:, :], tmp_a[:, :], float(SKIP), None, ALU.add))
            dve.wait_ge(turned_loaded, 16 * (GT + 1))
            v.tensor_copy(first_idx[:, :], first_head[:, :])
            dve.wait_ge(dis_turned, 1)
            link(v.tensor_copy(cc[:, :, 1], psR[:, 0:TILES]))
            v.tensor_tensor(cc[:, :, 2], cc[:, :, 1], cc[:, :, 1], ALU.mult)
            dve.wait_ge(attr_loaded, 16 * (DE + 1))
            v.tensor_tensor(attr_s[:, :], attr_s[:, :], root_s[:, :], ALU.mult).then_inc(attr_scaled, 1)

            L2 = slice((LAYERS - 1) * D, LAYERS * D)
            link(v.bn_stats(stats[:, 0:6], last_bias[:, :]))
            link(v.bn_aggr(mv[:, 0:2], stats[:, 0:6]))
            v.engine_nop().then_inc(var_ready, 1)
            dve.wait_ge(root_ready, 2)
            link(v.reciprocal(sc[:, 0:1], sc[:, 2:3]))
            link(v.scalar_tensor_tensor(base[:, :], last_bias[:, :], mv[:, 0:1], ln_w[:, L2], ALU.subtract, ALU.mult))
            link(v.scalar_tensor_tensor(base[:, :], base[:, :], sc[:, 0:1], ln_b[:, L2], ALU.mult, ALU.add))
            link(v.tensor_scalar(base[:, :], base[:, :], 0.0, None, ALU.max))

            def add_base(q):
                xi, xo = (part(buf, q, CW)[0:XP, :].rearrange("p (r d) -> p r d", d=D) for buf in (xin, xout))
                bb = base[0:XP, :].rearrange("p (o d) -> p o d", o=1).broadcast_to([XP, CR, D])
                v.tensor_tensor(xo, xi, bb, ALU.add).then_inc(x_based.sem, 1)

            for q in range(2):
                dve.wait_ge(x_in[q], 16)
                add_base(q)
            with dve.Fori(0, ITERS) as i:
                for q in range(2):
                    n = i * 2 + q
                    dve.wait_ge(dup_rows[q], i * 16 + 16)
                    dve.wait_ge(dup_done.sem, dup_done.done(n) - 1)
                    for b in range(GT):
                        ins = v.scalar_tensor_tensor(
                            junk[:, b * GE:(b + 1) * GE], part(rows_src, q), src_f[:, bass.ds(n * GT + b, 1)],
                            before[:, b * GE:(b + 1) * GE], ALU.is_equal, ALU.mult,
                            accum_out=earlier[:, bass.ds(n * GT + b, 1)])
                    ins.then_inc(dup_done.sem, 1)
                    dve.wait_ge(x_in[q], i * 16 + 32)
                    dve.wait_ge(base_out[q], i * 16 + 16)
                    add_base(q)
            dve.wait_ge(dup_done.sem, dup_done.done(GROUPS - 1))
            v.tensor_tensor(tmp_a[:, :], src_f[:, :], dump_a[:, :], ALU.subtract)
            link(v.tensor_scalar(earlier[:, :], earlier[:, :], 0.0, None, ALU.is_equal))
            link(v.tensor_tensor(tmp_a[:, :], tmp_a[:, :], earlier[:, :], ALU.mult))
            link(v.tensor_tensor(add_idx[:, :], tmp_a[:, :], dump_a[:, :], ALU.add))
            v.engine_nop().then_inc(idx_ready, 1)

            for l in range(LAYERS):
                first, last = l == 0, l == LAYERS - 1
                LW = slice(l * D, (l + 1) * D)
                K = (14, 8, 16)[l]
                turn = [None, 0, 0]

                def mark(ins):
                    if turn[0] is None:
                        chain[0] += 1
                        value = chain[0]
                    else:
                        turn[2] += 1
                        value = turn[0] * K + (chain[0] - turn[1] * K + turn[2])
                    ins.then_inc(dve_step, 1)
                    return value

                def after(value, alone=False):
                    settle(dve_step, value, alone)

                def step(ins, alone=False):
                    after(mark(ins), alone)

                def settle(s, value, alone=True):
                    if alone and not isinstance(value, int):
                        value = dve.to_reg(value)
                        dve.wait_ge(credits_, 1)
                    dve.wait_ge(s, value)

                def mvs(q):
                    return part(mv, q, 2 * GT).rearrange("p (b k) -> p b k", k=2)

                def scs(q):
                    return part(sc, q, 2 * GT).rearrange("p (b k) -> p b k", k=2)

                def scalars(i, q, c):
                    return cols[:, bass.ds(i * (-8 * GT) + (GROUPS - 1 - q) * (4 * GT), 4 * GT)].rearrange(
                        "p (b k) -> p b k", k=4)[:, :, c]

                def col(buf, q, b, c, w):
                    at = (q * GT + b) * w + c
                    return buf[:, at:at + 1]

                def row_stats(buf, q):
                    for b in range(GT):
                        ins = v.bn_stats(rstats[:, 6 * b:6 * b + 6], cut(buf, q, b))
                    return mark(ins)

                def row_vars(q, value):
                    after(value, alone=True)
                    r = part(rmv, q, 2 * GT).rearrange("p (b k) -> p b k", k=2)
                    for b in range(GT):
                        ins = v.bn_aggr(r[:, b, :], rstats[:, 6 * b:6 * b + 6])
                    ins.then_inc(row_var.sem, 1)

                def row_scales(q, at, done, extra):
                    r = part(rmv, q, 2 * GT).rearrange("p (b k) -> p b k", k=2)
                    s2 = part(rsc, q, 2 * GT).rearrange("p (b k) -> p b k", k=2)
                    dve.wait_ge(row_root.sem, row_root.done(at))
                    step(v.reciprocal(s2[:, :, 0], s2[:, :, 0]))
                    if extra is not None:
                        dve.wait_ge(own_in[q], extra)
                        own_dis = part(stage_row, q, 2 * GT).rearrange("p (b k) -> p b k", k=2)[:, :, 1]
                        step(v.tensor_tensor(s2[:, :, 0], s2[:, :, 0], own_dis, ALU.mult))
                    v.scalar_tensor_tensor(s2[:, :, 1], r[:, :, 0], -1.0, s2[:, :, 0],
                                           ALU.mult, ALU.mult).then_inc(done.sem, 1)

                def norm_stats(i, q):
                    dve.wait_ge(g_ready.sem, g_ready.free(G(l, i, q)))
                    dve.wait_ge(gathered[q], i * (16 * GT) + 16 * GT)
                    return row_stats(gat, q)

                def columns(i, q):
                    return mark(v.tensor_copy(part(stage_cols, q, 4 * GT),
                                              cols[:, bass.ds(i * (-8 * GT) + (GROUPS - 1 - q) * (4 * GT), 4 * GT)]))

                def equal(i, q, bs):
                    n = G(l, i, q)
                    if bs[0] == GT - 1:
                        dve.wait_ge(rows_in[q], i * 16 + (16 * (ITERS * l + 1)))
                        dve.wait_ge(U_done.sem, U_done.free(n))
                    for b in bs:
                        ins = v.tensor_scalar(cut(eq, q, b), cut(rows, q, b), col(stage_cols, q, b, 0, 4),
                                              None, ALU.is_equal)
                    if bs[-1] == 0:
                        ins.then_inc(eq_ready.sem, 1)

                def join(i, q):
                    n = G(l, i, q)
                    dve.wait_ge(zr_ready.sem, zr_ready.done(G(l - 1, i, q)))
                    for b in reversed(range(GT)):
                        zb = z[:, b * P:(b + 1) * P]
                        ins = v.scalar_tensor_tensor(cut(z2, q, b), psH[:, b * P:(b + 1) * P],
                                                     col(stage_cols, q, b, 3, 4), zb, ALU.mult, ALU.add)
                    ins.then_inc(z_ready.sem, 1)

                def take(i, q, s):
                    b = GT - 1 - s
                    dve.wait_ge(U_done.sem, U_done.done(G(l, i, q), s + 1))
                    v.tensor_copy(carry[0:1, LW], sums(q, b, 1)).then_inc(carried.sem, 1)
                    v.bn_stats(stats[:, 6 * b:6 * b + 6], sums(q, b)).then_inc(stat_done.sem, 1)

                def sum_vars(i, q):
                    n = G(l, i, q)
                    settle(stat_done.sem, stat_done.done(n))
                    for b in range(GT):
                        ins = v.bn_aggr(mvs(q)[:, b, :], stats[:, 6 * b:6 * b + 6])
                    step(ins)
                    if not last:
                        dve.wait_ge(act_done.sem, act_done.free(n))
                    v.tensor_tensor(scs(q)[:, :, 0], mvs(q)[:, :, 1], scalars(i, q, 2), ALU.mult
                                    ).then_inc(sum_var.sem, 1)

                def scale1(i, q):
                    dve.wait_ge(sum_root.sem, sum_root.done(G(l, i, q)))
                    return mark(v.reciprocal(scs(q)[:, :, 0], scs(q)[:, :, 0]))

                def scale2(i, q):
                    return mark(v.tensor_tensor(scs(q)[:, :, 0], scs(q)[:, :, 0], scalars(i, q, 1), ALU.mult))

                def scale3(i, q):
                    v.scalar_tensor_tensor(scs(q)[:, :, 1], mvs(q)[:, :, 0], -1.0, scs(q)[:, :, 0],
                                           ALU.mult, ALU.mult).then_inc(y_ready.sem, 1)

                def centred(i, q):
                    for b in range(GT):
                        ins = v.scalar_tensor_tensor(cut(y, q, b), sums(q, b), col(mv, q, b, 0, 2),
                                                     ln_w[:, LW], ALU.subtract, ALU.mult)
                    ins.then_inc(U_free.sem, 1)

                def affine(i, q):
                    dve.wait_ge(U_free.sem, U_free.done(i * 2 + q))
                    for b in range(GT):
                        ins = v.scalar_tensor_tensor(cut(y, q, b), cut(y, q, b), col(sc, q, b, 0, 2),
                                                     ln_b[:, LW], ALU.mult, ALU.add)
                    return mark(ins)

                def make_x1(i, q):
                    dve.wait_ge(xd_loaded[q], i * 16 + 16)
                    if shift(i, q, -2):
                        dve.wait_ge(x1_out[q], i * (16 * GT))
                    dve.wait_ge(zz_ready.sem, zz_ready.free(i * 2 + q))
                    return mark(v.scalar_tensor_tensor(part(x1, q), part(y, q), 0.0, part(xd, q), ALU.max, ALU.add))

                def one(i, q):
                    this, before, before2, nx, rows3 = (shift(i, q, d) for d in (0, -1, -2, 1, 3))
                    rows3 = rows3 if first else None
                    if nx:
                        value = columns(*nx)
                    if this:
                        take(*this, 0)
                    if nx:
                        after(value)
                        equal(*nx, (3, 2))
                    if before:
                        value = scale1(*before)
                    if this:
                        take(*this, 1)
                    if before:
                        after(value)
                        value = scale2(*before)
                    if nx:
                        equal(*nx, (1, 0))
                    if last and before2:
                        row_scales(before2[1], before2[0] * 2 + (GROUPS + before2[1]), x1_ready, None)
                    if before:
                        after(value)
                        if last:
                            centred(*before)
                        else:
                            scale3(*before)
                    if this:
                        take(*this, 2)
                    if rows3:
                        r_value = norm_stats(*rows3)
                    if nx and not first:
                        join(*nx)
                    if last and before:
                        y_value = affine(*before)
                    if rows3:
                        row_vars(rows3[1], r_value)
                    if this:
                        take(*this, 3)
                    if last and before:
                        after(y_value)
                        after(make_x1(*before), alone=True)
                        r_value = row_stats(x1, before[1])
                    if rows3:
                        row_scales(rows3[1], G(l, *rows3), normed, rows3[0] * (16 * GT) + 16 * GT)
                    if this:
                        sum_vars(*this)
                    if last and before:
                        row_vars(before[1], r_value)

                def body(i, lo):
                    turn[:] = [i, lo, 0] if lo is not None else [None, 0, 0]
                    for q in range(2):
                        one(i, q)
                    if lo is not None:
                        assert turn[2] == K, (l, turn[2])
                        chain[0] += K * (ITERS - 2 - lo)

                if last:
                    dve.wait_ge(act_done.sem, act_done.done(GROUPS * l - 1))
                bodies(dve, body, last)
                if first:
                    dve.wait_ge(own_kept.sem, own_kept.done(GROUPS - 1))
                    ow = own[:, :].rearrange("p (c k) -> p c k", k=2)
                    link(v.tensor_copy(src_row_idx[:, :], ow[:, :, 0]))
                    link(v.tensor_copy(cc[:, :, 3], ow[:, :, 1]))
                    v.engine_nop().then_inc(srcs_ready, 1)

            start = chain[0]
            with dve.Fori(0, ITERS) as i:
                for q in range(2):
                    n = i * 2 + q
                    dve.wait_ge(m_ready.sem, m_ready.free(n))
                    v.tensor_copy(part(stage_cols, q, 4 * GT),
                                  cols_out[:, bass.ds(n * (4 * GT), 4 * GT)]).then_inc(dve_step, 1)
                    dve.wait_ge(dve_step, n + (start + 1))
                    dve.wait_ge(v_loaded[q], i * 48 + 48)
                    dve.wait_ge(C_done.sem, C_done.free(n))
                    for b in range(GT):
                        c0 = (q * GT + b) * 4
                        v.tensor_scalar(cut(eq, q, b), cut(rows, q, b), stage_cols[:, c0:c0 + 1],
                                        stage_cols[:, c0 + 1:c0 + 2], ALU.is_equal, ALU.mult)
                        ins = v.tensor_scalar(cut(same_src, q, b, GE), part(rows_src, q),
                                              stage_cols[:, c0 + 2:c0 + 3], None, ALU.is_equal)
                    ins.then_inc(eqs_ready.sem, 1)

        @block.scalar
        def _(act):
            a = nc.scalar
            act.wait_ge(credits_, 1)
            act.wait_ge(pool_step, 1)
            act.wait_ge(var_ready, 1)
            a.activation(root_b[:, :], deg_b[:, :], ACT.Sqrt).then_inc(root_ready, 1)
            act.wait_ge(var_ready, 2)
            a.activation(sc[:, 2:3], mv[:, 1:2], ACT.Sqrt, bias=eps[:, :]).then_inc(root_ready, 1)
            def roots(done, to, var, q):
                s = part(to, q, 2 * GT).rearrange("p (b k) -> p b k", k=2)[:, :, 0]
                a.activation(s, var, ACT.Sqrt, bias=eps[:, :]).then_inc(done.sem, 1)

            def second(buf, q, c):
                return part(buf, q, 2 * GT).rearrange("p (b k) -> p b k", k=2)[:, :, c]

            for l in range(LAYERS):
                first, last = l == 0, l == LAYERS - 1
                table = v_tab if last else h_tab[l]

                def norm_root(i, q):
                    act.wait_ge(row_var.sem, row_var.done(G(l, i, q)))
                    roots(row_root, rsc, second(rmv, q, 1), q)

                def norm(i, q):
                    act.wait_ge(normed.sem, normed.done(G(l, i, q)))
                    act.wait_ge(T_done.sem, T_done.free(G(l, i, q)))
                    for b in range(GT):
                        c = (q * GT + b) * 2
                        ins = a.activation(cut(x_normed, q, b), cut(gat, q, b), ACT.Relu,
                                           bias=rsc[:, c + 1:c + 2], scale=rsc[:, c:c + 1])
                    ins.then_inc(g_ready.sem, 1)
                    act.wait_ge(own_in[q], i * (16 * GT) + 16 * GT)
                    a.copy(own[:, bass.ds(i * (-4 * GT) + (GROUPS - 1 - q) * (2 * GT), 2 * GT)],
                           part(stage_row, q, 2 * GT)).then_inc(own_kept.sem, 1)

                def turned(i, q):
                    act.wait_ge(T_done.sem, T_done.done(G(l, i, q)))
                    if first:
                        a.copy(part(hT, q), psT[:, :]).then_inc(hT_ready.sem, 1)
                    else:
                        a.activation(part(hT, q), psT[:, :], ACT.Relu, bias=ln_cols[:, LAYERS + l - 1:LAYERS + l],
                                     scale=ln_cols[:, l - 1:l]).then_inc(hT_ready.sem, 1)

                def mlp(i, q):
                    act.wait_ge(R_done.sem, R_done.done(G(l, i, q)))
                    a.activation(part(rT, q), psR[:, :], ACT.Relu).then_inc(rT_ready.sem, 1)

                def keep_z(i, q):
                    n = G(l, i, q)
                    act.wait_ge(Z_done.sem, Z_done.done(n))
                    if first:
                        act.wait_ge(U_done.sem, U_done.free(n))
                        a.copy(part(z2, q), psZ[:, :]).then_inc(z_ready.sem, 1)
                    else:
                        act.wait_ge(z_ready.sem, z_ready.done(n) - 1)
                        a.copy(z[:, :], psZ[:, :]).then_inc(zr_ready.sem, 1)

                def store(i, q):
                    act.wait_ge(act_done.sem, act_done.done(G(l, i, q)))
                    act.dma_start(
                        table[1:EP + 1, :].rearrange("(c p) d -> p c d", p=P)[
                            :, bass.ds(i * (-2 * GT) + (GROUPS - 1 - q) * GT, GT), :],
                        part(ho, q).rearrange("p (b d) -> p b d", b=GT)).then_inc(stored[q], 16)

                def sum_roots(i, q):
                    act.wait_ge(sum_var.sem, sum_var.done(G(l, i, q)))
                    roots(sum_root, sc, second(sc, q, 0), q)

                def keep_normed(i, q):
                    act.wait_ge(y_ready.sem, y_ready.done(G(l, i, q)))
                    act.wait_ge(stored[q], i * 16 + (16 + 16 * ITERS * l))
                    for b in range(GT):
                        c = (q * GT + b) * 2
                        ins = a.activation(cut(ho, q, b), sums(q, b), ACT.Identity,
                                           bias=sc[:, c + 1:c + 2], scale=sc[:, c:c + 1])
                    ins.then_inc(act_done.sem, 1)
                    store(i, q)

                def x1_root(i, q):
                    act.wait_ge(row_var.sem, row_var.done(i * 2 + (GROUPS + q)))
                    roots(row_root, rsc, second(rmv, q, 1), q)

                def x1_norm(i, q):
                    act.wait_ge(x1_ready.sem, x1_ready.done(i * 2 + q))
                    act.wait_ge(T2_done.sem, T2_done.free(i * 2 + q))
                    for b in range(GT):
                        c = (q * GT + b) * 2
                        ins = a.activation(cut(zz, q, b), cut(x1, q, b), ACT.Relu,
                                           bias=rsc[:, c + 1:c + 2], scale=rsc[:, c:c + 1])
                    ins.then_inc(zz_ready.sem, 1)

                def turned_x1(i, q):
                    act.wait_ge(T2_done.sem, T2_done.done(i * 2 + q))
                    a.copy(zT[:, :], psT[:, :]).then_inc(zT_ready.sem, 1)

                def keep_v(i, q):
                    act.wait_ge(V_done.sem, V_done.done(i * 2 + q))
                    act.wait_ge(stored[q], i * 16 + (16 + 16 * ITERS * l))
                    a.copy(part(ho, q), psR[:, :]).then_inc(act_done.sem, 1)
                    store(i, q)

                def one(i, q):
                    this, before, before2, before3, nx, nx2, rows3 = (shift(i, q, d) for d in (0, -1, -2, -3, 1, 2, 3))
                    rows3 = rows3 if first else None
                    if before and not last:
                        keep_normed(*before)
                    if before3 and last:
                        turned_x1(*before3)
                    if nx:
                        keep_z(*nx)
                    if before3 and last:
                        keep_v(*before3)
                    if before2 and last:
                        x1_norm(*before2)
                    if nx2:
                        turned(*nx2)
                        mlp(*nx2)
                    if rows3:
                        norm_root(*rows3)
                    if this:
                        sum_roots(*this)
                    if rows3:
                        norm(*rows3)
                    if last and before:
                        x1_root(*before)

                def body(i, lo):
                    for q in range(2):
                        one(i, q)

                bodies(act, body, last)

            for q in range(2):
                act.wait_ge(stored[q], 16 + 16 * ITERS * LAYERS)
            with act.Fori(0, ITERS) as i:
                for q in range(2):
                    n = i * 2 + q
                    act.wait_ge(M_done.sem, M_done.done(n))
                    for b in range(GT):
                        c = (q * GT + b) * 4 + 3
                        ins = a.activation(z[:, b * P:(b + 1) * P], psZ[:, b * P:(b + 1) * P], ACT.Copy,
                                           scale=stage_cols[:, c:c + 1])
                    ins.then_inc(m_ready.sem, 1)
                    act.wait_ge(C_done.sem, C_done.done(n))
                    act.wait_ge(staged, n + (STAGED_BEFORE + 1))
                    a.copy(part(ho, q), psT[:, :]).then_inc(c_ready.sem, 1)

        @block.tensor
        def _(pe):
            T = nc.tensor
            pe.wait_ge(credits_, 1)
            pe.wait_ge(loaded, 16 * 24)
            pe.wait_ge(seam_up, 1)
            T.transpose(psS[0:1, 0:P], seam[:, 0:1], ident[:, :])
            T.transpose(psS[0:1, P:2 * P], seam[:, 1:2], ident[:, :]).then_inc(seam_flat, 1)
            pe.wait_ge(seam_up, 2)
            T.matmul(psS[:, 2 * P:2 * P + 1], seam_row[0:1, 2 * P:3 * P], ident[0:1, 0:1], start=True, stop=True)
            T.matmul(psS[:, 2 * P + 1:2 * P + 2], seam_row[0:1, 3 * P:4 * P], ident[0:1, 0:1],
                     start=True, stop=True).then_inc(seam_down, 1)
            pe.wait_ge(turned_loaded, 16 * (GT + 1))
            for j in range(GT):
                ins = T.transpose(psR[:, j * TQ:(j + 1) * TQ], dis_t[:, j * P:(j + 1) * P], ident[0:TQ, 0:TQ])
            ins.then_inc(dis_turned, 1)

            pe.wait_ge(idx_ready, 1)
            for l in range(LAYERS):
                first, last = l == 0, l == LAYERS - 1
                LW = slice(l * D, (l + 1) * D)

                def turn(i, q):
                    n = G(l, i, q)
                    if first:
                        pe.wait_ge(g_ready.sem, g_ready.done(n))
                    else:
                        pe.wait_ge(gathered[q], i * (16 * GT) + (16 * GT * (ITERS * l + 1)))
                    pe.wait_ge(hT_ready.sem, hT_ready.done(n) - 1)
                    for b in range(GT):
                        ins = T.transpose(psT[:, b * P:(b + 1) * P], cut(x_normed if first else gat, q, b), ident[:, :])
                    ins.then_inc(T_done.sem, 1)

                def mlp(i, q):
                    n = G(l, i, q)
                    pe.wait_ge(rT_ready.sem, rT_ready.done(n) - 1)
                    held = i * 16 + (16 * (ITERS * l + 1))
                    held = held if isinstance(held, int) else pe.to_reg(held)
                    pe.wait_ge(credits_, 1)
                    pe.wait_ge(attr_in[q], held)
                    T.matmul(psR[:, :], edge_w1[:, LW], part(attr, q), start=True, stop=True).then_inc(R_done.sem, 1)

                def per_edge(i, q, bs):
                    n = G(l, i, q)
                    if bs[0] == GT - 1:
                        pe.wait_ge(hT_ready.sem, hT_ready.done(n))
                        pe.wait_ge(rT_ready.sem, rT_ready.done(n))
                        pe.wait_ge(z_ready.sem, z_ready.done(n) - 1)
                        if not first:
                            pe.wait_ge(zr_ready.sem, zr_ready.done(G(l - 1, i, q)) - 1)
                    for b in bs:
                        zb = psZ[:, b * P:(b + 1) * P]
                        hb = zb if first else psH[:, b * P:(b + 1) * P]
                        T.matmul(hb, cut(hT, q, b), lin_w[:, LW], start=True, stop=not first)
                        ins = T.matmul(zb, cut(rT, q, b), edge_w2[:, LW], start=not first, stop=True)
                    if bs[-1] == 0:
                        ins.then_inc(Z_done.sem, 1)

                def tile_sum(i, q, s):
                    n, b = G(l, i, q), GT - 1 - s
                    if s == 0:
                        pe.wait_ge(z_ready.sem, z_ready.done(n))
                        pe.wait_ge(eq_ready.sem, eq_ready.done(n))
                        pe.wait_ge(rank3_in[q], i * 16 + (16 * (ITERS * l + 1)))
                        if last:
                            pe.wait_ge(U_free.sem, U_free.free(i * 2 + q))
                        else:
                            pe.wait_ge(act_done.sem, act_done.free(n))
                    if s >= 2:
                        pe.wait_ge(stat_done.sem, stat_done.done(n, s - 1))
                    T.matmul(sums(q, b), cut(eq, q, b), cut(z2, q, b), start=True, stop=False)

                def tile_carry(i, q, s):
                    n, b = G(l, i, q), GT - 1 - s
                    value = carried.done(n, s)
                    value = value if isinstance(value, int) else pe.to_reg(value)
                    pe.wait_ge(credits_, 1)
                    pe.wait_ge(carried.sem, value)
                    T.matmul(sums(q, b), rank3[:, (q * GT + b) * P:(q * GT + b + 1) * P], carry[:, LW],
                             start=False, stop=True).then_inc(U_done.sem, 1)

                def turn_x1(i, q):
                    pe.wait_ge(zz_ready.sem, zz_ready.done(i * 2 + q))
                    for b in range(GT):
                        ins = T.transpose(psT[:, b * P:(b + 1) * P], cut(zz, q, b), ident[:, :])
                    ins.then_inc(T2_done.sem, 1)

                def make_v(i, q):
                    pe.wait_ge(zT_ready.sem, zT_ready.done(i * 2 + q))
                    pe.wait_ge(act_done.sem, act_done.done(G(l, i, q)) - 1)
                    for b in range(GT):
                        ins = T.matmul(psR[:, b * P:(b + 1) * P], zT[:, b * P:(b + 1) * P], out_w[:, :],
                                       start=True, stop=True)
                    ins.then_inc(V_done.sem, 1)

                def one(i, q):
                    this, before3, nx, nx2 = (shift(i, q, d) for d in (0, -3, 1, 2))
                    before3 = before3 if last else None
                    if this:
                        tile_sum(*this, 0)
                        tile_carry(*this, 0)
                        tile_sum(*this, 1)
                    if before3:
                        if nx:
                            pe.wait_ge(hT_ready.sem, hT_ready.done(G(l, *nx)))
                        turn_x1(*before3)
                    if nx:
                        per_edge(*nx, (3, 2))
                    if this:
                        tile_carry(*this, 1)
                        tile_sum(*this, 2)
                    if nx:
                        per_edge(*nx, (1, 0))
                    if before3:
                        make_v(*before3)
                    if this:
                        tile_carry(*this, 2)
                        tile_sum(*this, 3)
                    if this and last:
                        tile_carry(*this, 3)
                    if nx2:
                        turn(*nx2)
                        if before3:
                            pe.wait_ge(act_done.sem, act_done.done(G(l, *before3)))
                        mlp(*nx2)
                    if this and not last:
                        tile_carry(*this, 3)

                def body(i, lo):
                    for q in range(2):
                        one(i, q)

                bodies(pe, body, last)

            with pe.Fori(0, ITERS) as i:
                for q in range(2):
                    n = i * 2 + q
                    pe.wait_ge(v_loaded[q], i * 48 + 48)
                    pe.wait_ge(eqs_ready.sem, eqs_ready.done(n))
                    pe.wait_ge(m_ready.sem, m_ready.done(n) - 1)
                    for b in range(GT):
                        ins = T.matmul(psZ[:, b * P:(b + 1) * P], cut(eq, q, b), cut(v_in, q, b), start=True, stop=True)
                    ins.then_inc(M_done.sem, 1)
                    pe.wait_ge(m_ready.sem, m_ready.done(n))
                    pe.wait_ge(c_ready.sem, c_ready.done(n) - 1)
                    for b in range(GT):
                        for k in range(GT):
                            s0 = (q * GT + k) * GE + b * P
                            ins = T.matmul(psT[:, b * P:(b + 1) * P], same_src[:, s0:s0 + P],
                                           z[:, k * P:(k + 1) * P], start=(k == 0), stop=(k == GT - 1))
                    ins.then_inc(C_done.sem, 1)


def kernel(x, src, dst, edge_attr_16, edge_weight, L0_gnn_lin_w, L0_gnn_edge_w1, L0_gnn_edge_b1, L0_gnn_edge_w2,
           L0_gnn_edge_b2, L0_gnn_bias, L0_gnn_ln_w, L0_gnn_ln_b, L1_gnn_W):
    import numpy as np
    import concourse.bacc as bacc
    from concourse import mybir as mb
    from concourse.bass_utils import run_bass_kernel_spmd

    def padded(a, fill):
        return np.concatenate([a, np.full((EP - E,) + a.shape[1:], fill, a.dtype)])

    def lay_a(a):
        return np.ascontiguousarray(a.reshape(TILES, P).T)

    def lay_b(a):
        return np.ascontiguousarray(a.reshape(P, TILES))

    src, dst = (np.asarray(a) for a in (src, dst))
    src_p, dst_p = padded(src, N), padded(dst, N)
    none = np.full((1,), -1, dst.dtype)
    prev, after = np.concatenate([none, dst_p[:-1]]), np.concatenate([dst_p[1:], none])
    pos = np.arange(EP, dtype=np.float32)
    tile0 = np.arange(TILES, dtype=np.float32).repeat(P) * P
    c = np.arange(GE)
    before = (c[None, None, :] < (c.reshape(GT, P).T)[:, :, None]).astype(np.float32).reshape(P, GT * GE)
    arrays = {
        "x": np.ascontiguousarray(x),
        "src_a": lay_a(src_p), "dst_a": lay_a(dst_p), "dst_a_prev": lay_a(prev),
        "ew_a": lay_a(padded(np.asarray(edge_weight), 0.0)),
        "dump_a": lay_a(np.tile(np.arange(GE, dtype=np.float32) + DUMP, GROUPS)),
        "dst_b": lay_b(dst_p), "dst_b_prev": lay_b(prev), "dst_b_next": lay_b(after),
        "pos_b": np.stack([lay_b(pos + 1), lay_b(tile0 + 1), lay_b(tile0 + P)]),
        "dst_row": dst_p[None, :], "src_row": src_p[None, :],
        "attr_t": np.ascontiguousarray(padded(np.asarray(edge_attr_16), 0.0).T),
        "lin_w": np.ascontiguousarray(L0_gnn_lin_w), "edge_w2": np.ascontiguousarray(L0_gnn_edge_w2),
        "edge_w1": np.concatenate([np.asarray(L0_gnn_edge_w1), np.asarray(L0_gnn_edge_b1)[:, None, :]], axis=1),
        "edge_b2": np.ascontiguousarray(L0_gnn_edge_b2), "bias": np.ascontiguousarray(L0_gnn_bias),
        "ln_w": np.ascontiguousarray(L0_gnn_ln_w), "ln_b": np.ascontiguousarray(L0_gnn_ln_b),
        "out_w": np.ascontiguousarray(L1_gnn_W),
        "ident": np.eye(P, dtype=np.float32), "before": before,
    }
    nc = bacc.Bacc("TRN2", target_bir_lowering=False, num_devices=1)
    t = {k: nc.dram_tensor(f"in_{k}", a.shape, mb.dt.from_np(a.dtype), kind="ExternalInput").ap()
         for k, a in arrays.items()}
    t["out"] = nc.dram_tensor("out", (ROWS_OUT, D), mb.dt.float32, kind="ExternalOutput").ap()
    gnn(nc, t)
    r = run_bass_kernel_spmd(nc, [{f"in_{k}": a for k, a in arrays.items()}], core_ids=[0])
    return r.results[0]["out"][:N]
```
